# Optimizing a Trainium2 kernel written in Bass

```python
import numpy as np
import jax
import jax.numpy as jnp

def _softmax(x, axis=-1):
    return jax.nn.softmax(x, axis=axis)

def _gelu(x):
    return jax.nn.gelu(x, approximate=True)

def _silu(x):
    return jax.nn.silu(x)

def _sigmoid(x):
    return jax.nn.sigmoid(x)

def _layernorm(x, axis=-1, eps=1e-05):
    m = jnp.mean(x, axis=axis, keepdims=True)
    v = jnp.var(x, axis=axis, keepdims=True)
    return (x - m) / jnp.sqrt(v + eps)

def _scatter_add(tgt, idx, src, axis=0):
    return tgt.at[idx].add(src)

def _segment_sum(src, seg, n):
    return jax.ops.segment_sum(src, seg, n)
kernel_name = 'mk_gnn_preln_d2_gnn_r32_faad4d'

def setup_inputs(seed: int=0):
    np.random.seed(seed)
    _w = jnp.asarray

    def _rec_inputs():
        import jax
        import jax.numpy as jnp
        _gk = jax.random.key(seed)
        x = -0.0003713 + 1 * jax.random.normal(jax.random.fold_in(_gk, 1), (3125, 256), jnp.float32)
        src = jax.random.randint(jax.random.fold_in(_gk, 2), (50000,), 0, 3125, jnp.int32)
        dst = jnp.minimum((3125 * jax.random.uniform(jax.random.fold_in(_gk, 3), (50000,)) ** 2.0).astype(jnp.int32), 99999)
        _o = jnp.argsort(dst, stable=True)
        src = src[_o]
        dst = dst[_o]
        edge_type_8 = jax.random.randint(jax.random.fold_in(_gk, 12), (50000,), 0, 8, jnp.int32)
        return (x, src, dst, edge_type_8)
    x, src, dst, edge_type_8 = _rec_inputs()

    def _L0_gnn_setup():
        import jax, jax.numpy as jnp
        import numpy as np
        NUM_NODES = 50000
        NUM_EDGES = 25000
        NUM_REL = 8
        DIM = 256

        def _rgcn_conv(x, W, Wroot, b, src, dst, etype):
            N = x.shape[0]
            R = W.shape[0]
            xs = x[src]
            seg = dst * R + etype
            sums = jax.ops.segment_sum(xs, seg, num_segments=N * R)
            cnt = jax.ops.segment_sum(jnp.ones_like(xs[:, 0]), seg, num_segments=N * R)
            mean = sums / jnp.maximum(cnt, 1.0)[:, None]
            mean = mean.reshape(N, R, -1)
            return x @ Wroot + b + jnp.einsum('nrd,rde->ne', mean, W)
        key = jax.random.key(seed)
        ks = jax.random.split(key, 8)
        x = jax.random.normal(ks[0], (NUM_NODES, DIM), dtype=jnp.float32)
        edge_index = jax.random.randint(ks[1], (2, NUM_EDGES), 0, NUM_NODES, dtype=jnp.int64)
        edge_type = jax.random.randint(ks[2], (NUM_EDGES,), 0, NUM_REL, dtype=jnp.int64)
        s = 1.0 / np.sqrt(DIM)
        W1 = jax.random.normal(ks[3], (NUM_REL, DIM, DIM), dtype=jnp.float32) * s
        Wroot1 = jax.random.normal(ks[4], (DIM, DIM), dtype=jnp.float32) * s
        b1 = jnp.zeros((DIM,), dtype=jnp.float32)
        W2 = jax.random.normal(ks[5], (NUM_REL, DIM, DIM), dtype=jnp.float32) * s
        Wroot2 = jax.random.normal(ks[6], (DIM, DIM), dtype=jnp.float32) * s
        b2 = jnp.zeros((DIM,), dtype=jnp.float32)
        return {'x': x, 'edge_index': edge_index, 'edge_type': edge_type, 'W1': W1, 'Wroot1': Wroot1, 'b1': b1, 'W2': W2, 'Wroot2': Wroot2, 'b2': b2}
    _L0_gnn_all = _L0_gnn_setup()
    _L0_gnn_in = {k: v for k, v in _L0_gnn_all.items() if k in ('W1', 'Wroot1', 'b1', 'W2', 'Wroot2', 'b2')}
    del _L0_gnn_all

    def _L1_gnn_setup():
        import jax, jax.numpy as jnp
        import numpy as np
        N_NODES = 50000
        N_EDGES = 50000
        IN_DIM, OUT_DIM, N_HEADS = (256, 64, 4)
        EPS = 1e-12
        key = jax.random.key(seed)
        k1, k2, k3, k4, k5 = jax.random.split(key, 5)
        h = jax.random.normal(k1, (N_NODES, IN_DIM), dtype=jnp.float32)
        edge_index = jax.random.randint(k2, (2, N_EDGES), 0, N_NODES, dtype=jnp.int32)
        W = jax.random.normal(k3, (IN_DIM, OUT_DIM), dtype=jnp.float32) * 0.05
        Wl = jax.random.normal(k4, (N_HEADS, OUT_DIM), dtype=jnp.float32) * 0.05
        Wr = jax.random.normal(k5, (N_HEADS, OUT_DIM), dtype=jnp.float32) * 0.05
        b = jnp.zeros((OUT_DIM,), dtype=jnp.float32)
        return {'h': h, 'W': W, 'Wl': Wl, 'Wr': Wr, 'b': b, 'edge_index': edge_index}
    _L1_gnn_all = _L1_gnn_setup()
    _L1_gnn_in = {k: v for k, v in _L1_gnn_all.items() if k in ('W', 'Wl', 'Wr', 'b')}
    del _L1_gnn_all
    return {'x': x, 'src': src, 'dst': dst, 'edge_type_8': edge_type_8, 'L0_gnn_W1': _L0_gnn_in['W1'], 'L0_gnn_Wroot1': _L0_gnn_in['Wroot1'], 'L0_gnn_b1': _L0_gnn_in['b1'], 'L0_gnn_W2': _L0_gnn_in['W2'], 'L0_gnn_Wroot2': _L0_gnn_in['Wroot2'], 'L0_gnn_b2': _L0_gnn_in['b2'], 'L1_gnn_W': _L1_gnn_in['W'], 'L1_gnn_Wl': _L1_gnn_in['Wl'], 'L1_gnn_Wr': _L1_gnn_in['Wr'], 'L1_gnn_b': _L1_gnn_in['b']}

def reference(x, src, dst, edge_type_8, L0_gnn_W1, L0_gnn_Wroot1, L0_gnn_b1, L0_gnn_W2, L0_gnn_Wroot2, L0_gnn_b2, L1_gnn_W, L1_gnn_Wl, L1_gnn_Wr, L1_gnn_b):
    import jax
    import jax.numpy as jnp

    def _L0_gnn_ref(x, edge_index, edge_type, W1, Wroot1, b1, W2, Wroot2, b2):
        import jax, jax.numpy as jnp
        import numpy as np
        NUM_NODES = 50000
        NUM_EDGES = 25000
        NUM_REL = 8
        DIM = 256

        def _rgcn_conv(x, W, Wroot, b, src, dst, etype):
            N = x.shape[0]
            R = W.shape[0]
            xs = x[src]
            seg = dst * R + etype
            sums = jax.ops.segment_sum(xs, seg, num_segments=N * R)
            cnt = jax.ops.segment_sum(jnp.ones_like(xs[:, 0]), seg, num_segments=N * R)
            mean = sums / jnp.maximum(cnt, 1.0)[:, None]
            mean = mean.reshape(N, R, -1)
            return x @ Wroot + b + jnp.einsum('nrd,rde->ne', mean, W)
        src, dst = (edge_index[0], edge_index[1])
        h = _rgcn_conv(x, W1, Wroot1, b1, src, dst, edge_type)
        h = jax.nn.relu(h)
        h = _rgcn_conv(h, W2, Wroot2, b2, src, dst, edge_type)
        return h

    def _L1_gnn_ref(h, W, Wl, Wr, b, edge_index):
        import jax, jax.numpy as jnp
        import numpy as np
        N_NODES = 50000
        N_EDGES = 50000
        IN_DIM, OUT_DIM, N_HEADS = (256, 64, 4)
        EPS = 1e-12
        N = h.shape[0]
        H = Wl.shape[0]
        x = h @ W
        el = x @ Wl.T
        er = x @ Wr.T
        src, dst = (edge_index[0], edge_index[1])
        e = el[src] + er[dst]
        e = jnp.exp(jax.nn.leaky_relu(e, negative_slope=0.2))
        rowsum = jax.ops.segment_sum(e, src, num_segments=N)
        w = e / jnp.maximum(rowsum, EPS)[src]
        heads = [jax.ops.segment_sum(w[:, hd:hd + 1] * x[dst], src, num_segments=N) for hd in range(H)]
        out = jnp.stack(heads, axis=1)
        out = jax.nn.elu(out + b)
        return out.reshape(N, H * x.shape[1])
    edge_index = jnp.stack([src, dst])
    h = jnp.maximum(_layernorm(x, axis=-1), 0.0)
    x = x + _L0_gnn_ref(h, edge_index, edge_type_8, L0_gnn_W1, L0_gnn_Wroot1, L0_gnn_b1, L0_gnn_W2, L0_gnn_Wroot2, L0_gnn_b2)
    h = jnp.maximum(_layernorm(x, axis=-1), 0.0)
    x = x + _L1_gnn_ref(h, L1_gnn_W, L1_gnn_Wl, L1_gnn_Wr, L1_gnn_b, edge_index)
    return x

_drawn_inputs = setup_inputs


def setup_inputs(seed=0):
    import zlib

    import numpy as np

    out = dict(_drawn_inputs(seed))
    spreads = {'L0_gnn_b1': (0.0, 0.1), 'L0_gnn_b2': (0.0, 0.1), 'L1_gnn_b': (0.0, 0.1)}
    factors = {'L1_gnn_Wl': 8.0, 'L1_gnn_Wr': 8.0}
    for name, (base, spread) in spreads.items():
        noise = np.random.default_rng([zlib.crc32(name.encode()), seed]).standard_normal(out[name].shape)
        drawn = base * np.exp(spread * noise) if base else spread * noise
        out[name] = jnp.asarray(drawn.astype(out[name].dtype))
    for name, factor in factors.items():
        out[name] = (out[name] * factor).astype(out[name].dtype)
    return out
```

```python
from contextlib import ExitStack

import numpy as np

import concourse.bass as bass
from concourse import mybir

F32 = mybir.dt.float32
F16 = mybir.dt.float16
I32 = mybir.dt.int32
U8 = mybir.dt.uint8
ALU = mybir.AluOpType
ACT = mybir.ActivationFunctionType
PE = mybir.EngineType.PE
DVE = mybir.EngineType.DVE

P = 128
SHIFT = 7


def build_gnn(nc, x, src, dst, etype, W1, Wroot1, b1, W2, Wroot2, b2, Wg, Wl, Wr, bg, out):
    N, D = x.shape
    E = src.shape[0]
    R = W1.shape[0]
    OD, HEADS = Wg.shape[1], Wl.shape[0]
    TILES = -(-N // P)
    TAIL = N - (TILES - 1) * P
    KH = D // P
    EP = next(p for p in range(P, 0, -1) if E % p == 0)
    EC = E // EP
    CHUNKS = -(-(E // P + TILES) // 16) * 16
    GROUPS = CHUNKS // 4
    TURNS = GROUPS // 4
    assert CHUNKS >= EC and CHUNKS >= E // P + TILES and CHUNKS <= 512
    assert KH == 2 and HEADS * OD == D
    YC = R * D // 512
    HC = TILES * R
    TW = OD + HEADS
    AW = D + HEADS
    EPS_LN, EPS_ROW, SLOPE = 1e-5, 1e-12, 0.2

    y_dram = nc.dram_tensor("y_rows", (TILES * P * R, D), F32, kind="Internal").ap()
    tab_dram = nc.dram_tensor("attention_rows", (TILES * P, TW), F32, kind="Internal").ap()
    y_tiles = y_dram.rearrange("(t p r) d -> p t (r d)", p=P, r=R)
    tab_tiles = tab_dram.rearrange("(t p) c -> p t c", p=P)

    with ExitStack() as ctx:
        def sb(name, shape, dt):
            return ctx.enter_context(nc.sbuf_tensor(name, shape, dt))

        def sem(name):
            return ctx.enter_context(nc.semaphore(name))

        bank = [ctx.enter_context(nc.psum_tensor(f"bank{i}", [P, 512], F32)) for i in range(6)]
        turn16 = [ctx.enter_context(nc.psum_tensor(f"turn16_{i}", [P, 1024], F16)) for i in range(2)]
        small_ps, hist_ps = bank[4], bank[5]
        perm_ps = [t[:, :].bitcast(F32) for t in turn16]

        iota16 = sb("iota16", [P, 512], F16)
        lane_no = sb("lane_no", [P, 1], F32)
        ident = sb("ident", [P, P], F32)
        ident16 = sb("ident16", [P, P], F16)
        before = sb("before", [P, P], F32)
        ones = sb("ones", [P, P], F32)
        zeros = sb("zeros", [P, CHUNKS], U8)
        eps_col = sb("eps_col", [P, 1], F32)
        bias1 = sb("bias1", [P, D], F32)
        bias2 = sb("bias2", [P, D], F32)
        biasg = sb("biasg", [P, OD], F32)

        xb = sb("xb", [P, TILES * D], F32)
        acc = sb("acc", [P, TILES * AW], F32)
        hT = sb("hT", [P, KH, TILES * P], F32)
        w_sb = sb("w_sb", [P, KH, R * D], F32)
        wroot_sb = sb("wroot_sb", [P, KH, D], F32)
        stats = sb("stats", [P, TILES, 6], F32)
        mv = sb("mv", [P, TILES, 2], F32)
        rstd = sb("rstd", [P, TILES], F32)
        rcnt = sb("rcnt", [P, HC], F32)
        wg_sb = sb("wg_sb", [P, KH, OD], F32)
        head_w = sb("head_w", [OD, OD + 2 * HEADS], F32)
        x1T = sb("x1T", [OD, 512], F32)
        tabst = sb("tabst", [P, TILES, TW], F32)
        el_tab = sb("el_tab", [P, TILES * HEADS], F32)

        src_i = sb("src_i", [EP, EC], I32)
        dst_i = sb("dst_i", [EP, EC], I32)
        et_i = sb("et_i", [EP, EC], I32)
        scratch = sb("scratch", [P, 9 * CHUNKS], F32)

        def scratch_list(k, n=1):
            return scratch[0:EP, k * CHUNKS:(k + n) * CHUNKS]
        tmp_i, tmp2_i, low_i = (scratch_list(k).bitcast(I32) for k in range(3))
        tile_f, low_f, pos = (scratch_list(k) for k in range(3, 6))
        key_f = scratch_list(6)
        run = scratch_list(7, 2).rearrange("p (a c) -> p a c", a=2)
        n_in = sb("n_in", [EP, TILES], F32)
        tot_i = sb("tot_i", [P, TILES], I32)
        nch = sb("nch", [P, TILES], F32)
        cend = sb("cend", [P, TILES], F32)
        start = sb("start", [P, TILES], F32)
        tid_f = sb("tid_f", [1, CHUNKS], F32)

        class Order:
            pass
        orders = []
        for name in ("dst", "src"):
            o = Order()
            o.chunk = sb(f"{name}_chunk", [EP, CHUNKS], F32)
            o.lane = sb(f"{name}_lane", [EP, CHUNKS], F32)
            o.hi = sb(f"{name}_hi", [EP, CHUNKS], F32)
            o.lo = sb(f"{name}_lo", [EP, CHUNKS], F32)
            o.tid = sb(f"{name}_tid", [1, CHUNKS], I32)
            o.idx = sb(f"{name}_idx", [P, CHUNKS], I32)
            o.loc = sb(f"{name}_loc", [P, CHUNKS], F32)
            orders.append(o)
        by_dst, by_src = orders
        et_f = sb("et_f", [P, CHUNKS], F32)
        weight = sb("weight", [P, CHUNKS], F32)
        slot_i = sb("slot_i", [P, CHUNKS], I32)
        slot2_i = sb("slot2_i", [P, CHUNKS], I32)
        empty = sb("empty", [P, CHUNKS], F32)

        RP = 8
        wide = sb("wide", [EP, RP, CHUNKS], F16)
        lanes = sb("lanes", [EP, RP, P], F16)
        lanes_hi = sb("lanes_hi", [EP, RP, P], F16)
        lanes_lo = sb("lanes_lo", [EP, RP, P], F16)
        rows = sb("rows", [P, 16, D], F32)
        ystage = rows[:, :, :].rearrange("p s d -> p (s d)").rearrange("p (n w) -> p n w", w=512)
        arhs = scratch[:, 0:8 * AW].rearrange("p (s c) -> p s c", c=AW)
        arows = scratch[:, 8 * AW:8 * AW + 16 * TW].rearrange("p (s c) -> p s c", c=TW)
        idx_ring = sb("idx_ring", [P, 16], I32)
        low_ring = sb("low_ring", [EP, RP], F32)
        hots = sb("hots", [P, 24 * P], F32)
        hot16 = hots[:, 0:8 * P].bitcast(F16).rearrange("p (s n) -> p s n", n=P)
        hotT = hots[:, 8 * P:16 * P].rearrange("p (a n) -> p a n", a=2)
        hot = hots[:, 16 * P:24 * P].rearrange("p (s n) -> p s n", n=P)
        member = hots[0:EP, 0:TILES * CHUNKS // 4].bitcast(U8).rearrange("p (k c) -> p k c", c=CHUNKS)
        zbuf = sb("zbuf", [P, 2, 4, HEADS], F32)
        trash = sb("trash", [P, 4, R], F32)

        x_in, e_in, b_in = sem("x_in"), sem("e_in"), sem("b_in")
        w1_in, w2_in, wg_in = sem("w1_in"), sem("w2_in"), sem("wg_in")
        pool_const = sem("pool_const")
        dve_link = sem("dve_link")
        normed_st = sem("stats_done")
        sqrt_done = sem("sqrt_done")
        const_done = sem("const_done")
        normed = sem("normed")
        turned = sem("turned")
        hT_done = sem("hT_done")
        y_prod = sem("y_prod")
        y_out = sem("y_out")
        y_stored = [sem(f"y_stored{n}") for n in range(YC)]
        root_prod, root_added = sem("root_prod"), sem("root_added")
        counts_ready, counts_summed, counts_read = sem("counts_ready"), sem("counts_summed"), sem("counts_read")
        hist_wide, hist_lane, hist_used = sem("hist_wide"), sem("hist_lane"), sem("hist_used")
        rcnt_done = sem("rcnt_done")
        perm_wide, perm_lane = sem("perm_wide"), sem("perm_lane")
        perm_scaled, perm_used = sem("perm_scaled"), sem("perm_used")
        order_done = sem("order_done")
        idx_placed, low_placed, pool_passed = sem("idx_placed"), sem("low_placed"), sem("pool_passed")
        landed = [sem(f"landed{s}") for s in range(16)]
        hot_ready, turnT, hotT_done = sem("hot_ready"), sem("turnT"), sem("hotT_done")
        looked, picked, hot_w = sem("looked"), sem("picked"), sem("hot_w")
        summed1, added1 = sem("summed1"), sem("added1")
        hot2, summed2, added2 = sem("hot2"), sem("summed2"), sem("added2")
        x1_prod, x1_out, tab_prod, tab_out = sem("x1_prod"), sem("x1_out"), sem("tab_prod"), sem("tab_out")
        tab_stored = sem("tab_stored")
        hot3, turnT3, hotT3, looked3 = sem("hot3"), sem("turnT3"), sem("hotT3"), sem("looked3")
        z_sum, z_done, e_done, rhs_done = sem("z_sum"), sem("z_done"), sem("e_done"), sem("rhs_done")
        hot3_w, summed3, added3 = sem("hot3_w"), sem("summed3"), sem("added3")
        low_done, exp_done, out_done, out_stored = sem("low_done"), sem("exp_done"), sem("out_done"), sem("out_stored")

        def at_least(eng, s, value):
            if not (isinstance(value, int) and value <= 0):
                eng.wait_ge(s, value)

        def turns(eng, step, lag):
            for q in range(4):
                step(0, q)
            with eng.Fori(1, TURNS) as i:
                for q in range(4):
                    step(i, q)
            for q in range(lag):
                step(TURNS, q)

        def group(i, q, lag):
            i2, q2 = (i, q - lag) if q >= lag else (i - 1, q - lag + 4)
            there = not isinstance(i, int) or 0 <= 4 * i2 + q2 < GROUPS
            return there, 4 * i2 + q2, i2, q2

        def tile_ids(engine, o, g):
            _, ids = nc.values_load_multi_w_load_instructions(
                o.tid[0:1, bass.ds(4 * g, 4)], engines=[engine], min_val=0, max_val=TILES - 1,
                skip_runtime_bounds_check_because="the ids are clamped to TILES - 1 when they are made")
            return ids

        def node_tile(t, width=D):
            return bass.ds(t * width, width)

        block = ctx.enter_context(nc.Block())

        @block.sync
        def _(sp):
            sp.dma_start(dst_i[:, :], dst.rearrange("(p c) -> p c", p=EP)).then_inc(e_in, 16)
            sp.dma_start(src_i[:, :], src.rearrange("(p c) -> p c", p=EP)).then_inc(e_in, 16)
            sp.dma_start(et_i[:, :], etype.rearrange("(p c) -> p c", p=EP)).then_inc(e_in, 16)
            sp.wait_ge(const_done, 1)
            sp.dma_start(xb[:, 0:(TILES - 1) * D].rearrange("p (t d) -> p t d", d=D),
                         x[0:(TILES - 1) * P, :].rearrange("(t p) d -> p t d", p=P)).then_inc(x_in, 16)
            sp.dma_start(xb[0:TAIL, (TILES - 1) * D:], x[(TILES - 1) * P:, :]).then_inc(x_in, 16)

            def load_weights(W, Wroot, done):
                for k in range(KH):
                    sp.dma_start(w_sb[:, k, :].rearrange("p (r e) -> p r e", r=R),
                                 W[:, k * P:(k + 1) * P, :].rearrange("r p e -> p r e")).then_inc(done, 16)
                sp.dma_start(wroot_sb[:, :, :], Wroot.rearrange("(k p) e -> p k e", p=P)).then_inc(done, 16)

            load_weights(W1, Wroot1, w1_in)
            sp.dma_start(bias1[:, :], b1.unsqueeze(0).broadcast_to([P, D])).then_inc(b_in, 16)
            sp.dma_start(bias2[:, :], b2.unsqueeze(0).broadcast_to([P, D])).then_inc(b_in, 16)
            sp.dma_start(biasg[:, :], bg.unsqueeze(0).broadcast_to([P, OD])).then_inc(b_in, 16)
            sp.dma_start(wg_sb[:, :, :], Wg.rearrange("(k p) e -> p k e", p=P)).then_inc(wg_in, 16)
            with nc.allow_non_contiguous_dma(reason="two 64 x 4 matrices, turned"):
                sp.dma_start(head_w[:, OD:OD + HEADS], Wr.rearrange("h o -> o h")).then_inc(wg_in, 16)
                sp.dma_start(head_w[:, OD + HEADS:], Wl.rearrange("h o -> o h")).then_inc(wg_in, 16)

            def store_y(layer):
                with sp.Fori(0, TILES) as t:
                    for n in range(YC):
                        sp.wait_ge(y_out, (t + layer * TILES) * YC + n + 1)
                        sp.dma_start(y_tiles[:, bass.ds(t, 1), n * 512:(n + 1) * 512],
                                     ystage[:, n:n + 1, :]).then_inc(y_stored[n], 16)

            store_y(0)
            sp.wait_ge(root_prod, TILES)
            load_weights(W2, Wroot2, w2_in)
            sp.wait_ge(added1, CHUNKS)
            store_y(1)

            sp.wait_ge(tab_out, TILES)
            sp.dma_start(tab_tiles, tabst[:, :, :]).then_inc(tab_stored, 16)

            for t in range(0, TILES, 5):
                sp.wait_ge(out_done, t // 5 + 1)
                last = t + 5 >= TILES
                full = TILES - 1 - t if last else 5
                sp.dma_start(out[t * P:(t + full) * P, :].rearrange("(t p) d -> p t d", p=P),
                             xb[:, t * D:(t + full) * D].rearrange("p (t d) -> p t d", d=D)).then_inc(out_stored, 16)
                if last:
                    sp.dma_start(out[(TILES - 1) * P:, :], xb[0:TAIL, (TILES - 1) * D:]).then_inc(out_stored, 16)
            sp.wait_ge(out_stored, 16 * (-(-TILES // 5) + 1))

        @block.gpsimd
        def _(pool):
            pool.iota(iota16[:, :], [[1, 512]], base=0, channel_multiplier=0,
                      allow_small_or_imprecise_dtypes=True).then_inc(pool_const, 1)
            pool.iota(lane_no[:, :], [[1, 1]], base=0, channel_multiplier=1,
                      allow_small_or_imprecise_dtypes=True).then_inc(pool_const, 1)

            pool.wait_ge(pool_const, 2)
            pool.wait_ge(counts_ready, 1)
            def hist_lanes(i):
                at_least(pool, hist_used, i * RP)
                pool.tensor_copy(low_ring[:, :], low_f[:, bass.ds(i * RP, RP)]).then_inc(low_placed, 1)
                pool.wait_ge(low_placed, i + 1)
                pool.sem_inc(pool_passed, 1)
                for u in range(RP):
                    pool.tensor_scalar(lanes_hi[:, u, :], iota16[0:EP, 0:P], low_ring[:, u:u + 1],
                                       None, ALU.is_equal).then_inc(hist_lane, 1)
            hist_lanes(0)
            with pool.Fori(1, EC // RP) as i:
                hist_lanes(i)

            def gather(layer, o, table, ring, used):
                def step(i, q):
                    at_least(pool, used, 4 * i + q - 3)
                    pool.tensor_copy(idx_ring[:, 4 * q:4 * q + 4],
                                     o.idx[:, bass.ds(16 * i + 4 * q, 4)]).then_inc(idx_placed, 1)
                    pool.wait_ge(idx_placed, 4 * i + q + 1 + layer * GROUPS)
                    pool.sem_inc(pool_passed, 1)
                    for u in range(4):
                        s = 4 * q + u
                        pool.indirect_dma_start(
                            out=ring[:, s, :], out_offset=None, in_=table,
                            in_offset=bass.IndirectOffsetOnAxis(ap=idx_ring[:, s:s + 1], axis=0),
                        ).then_inc(landed[s], 16)
                turns(pool, step, 0)

            pool.wait_ge(order_done, 1)
            for n in range(YC):
                pool.wait_ge(y_stored[n], 16 * TILES)
            gather(0, by_dst, y_dram, rows, summed1)
            for n in range(YC):
                pool.wait_ge(y_stored[n], 32 * TILES)
            gather(1, by_dst, y_dram, rows, summed2)
            pool.wait_ge(order_done, 2)
            pool.wait_ge(tab_stored, 16)
            gather(2, by_src, tab_dram, arows, rhs_done)

        @block.tensor
        def _(pe):
            def turn_tiles(phase, source):
                for t in range(TILES):
                    at_least(pe, normed, t + 1 + phase * TILES)
                    at_least(pe, hT_done, t - 4 + phase * TILES)
                    for k in range(KH):
                        last = pe.transpose(bank[t % 5][:, k * P:(k + 1) * P],
                                            source[:, t * D + k * P:t * D + (k + 1) * P], ident[:, :])
                    last.then_inc(turned, 1)

            def products(layer, w_ready):
                pe.wait_ge(w_ready, 16 * (KH + 1))
                pe.wait_ge(hT_done, TILES * (layer + 1))
                for t in range(TILES):
                    for n in range(YC):
                        at_least(pe, y_out, (t + layer * TILES - 1) * YC + n + 1)
                        for k in range(KH):
                            last = pe.matmul(bank[n][:, :], hT[:, k, t * P:(t + 1) * P],
                                             w_sb[:, k, n * 512:(n + 1) * 512], start=(k == 0), stop=(k == KH - 1))
                        last.then_inc(y_prod, 1)
                pe.wait_ge(y_out, TILES * YC * (layer + 1))
                for t in range(TILES):
                    at_least(pe, root_added, t - 4 + layer * TILES)
                    for k in range(KH):
                        last = pe.matmul(bank[t % 5][:, 0:D], hT[:, k, t * P:(t + 1) * P],
                                         wroot_sb[:, k, :], start=(k == 0), stop=(k == KH - 1))
                    last.then_inc(root_prod, 1)

            def sum_counts(n):
                pe.wait_ge(counts_ready, 2 * n + 2)
                pe.matmul(small_ps[:, 0:TILES], ones[0:EP, :], n_in[:, :], start=True, stop=True)
                pe.matmul(small_ps[:, TILES:2 * TILES], before[0:EP, :], n_in[:, :],
                          start=True, stop=True).then_inc(counts_summed, 1)

            def permute(c, u, first, last):
                pe.wait_ge(perm_wide, c + 1)
                pe.wait_ge(perm_scaled, c + 1)
                pe.matmul(perm_ps[0][:, 0:CHUNKS], lanes_hi[:, u, :], wide[:, u, :], start=first, stop=last,
                          skip_group_check=True)
                pe.matmul(perm_ps[1][:, 0:CHUNKS], lanes_lo[:, u, :], wide[:, u, :], start=first, stop=last,
                          skip_group_check=True).then_inc(perm_used, 1)

            pe.wait_ge(const_done, 1)
            turn_tiles(0, acc)
            pe.wait_ge(hT_done, TILES)
            sum_counts(0)
            sum_counts(1)
            pe.wait_ge(counts_read, 2)
            products(0, w1_in)

            for u in range(RP):
                pe.wait_ge(hist_wide, u + 1)
                pe.wait_ge(hist_lane, u + 1)
                pe.matmul(hist_ps[:, 0:HC], lanes_hi[:, u, :], wide[:, u, 0:HC], start=(u == 0), stop=False,
                          skip_group_check=True).then_inc(hist_used, 1)
            with pe.Fori(1, EC // RP) as i:
                for u in range(RP):
                    pe.wait_ge(hist_wide, i * RP + u + 1)
                    pe.wait_ge(hist_lane, i * RP + u + 1)
                    pe.matmul(hist_ps[:, 0:HC], lanes_hi[:, u, :], wide[:, u, 0:HC], start=False, stop=False,
                              skip_group_check=True).then_inc(hist_used, 1)

            for u in range(RP):
                permute(u, u, u == 0, False)
            with pe.Fori(1, CHUNKS // RP) as i:
                for u in range(RP):
                    permute(i * RP + u, u, False, False)

            pe.wait_ge(rcnt_done, 1)
            pe.wait_ge(order_done, 1)

            def turn_hot(i, q, ready, out_done_):
                there, g, _, gq = group(i, q, 0)
                if there:
                    pe.wait_ge(ready, g + 1)
                    at_least(pe, out_done_, g - 1)
                    for u in range(4):
                        last = pe.transpose(turn16[gq % 2][:, u * P:(u + 1) * P], hot16[:, 4 * gq + u, :],
                                            ident16[:, :])
                    return last

            def step1(i, q):
                there, g, _, gq = group(i, q, 1)
                if there:
                    ids = tile_ids(PE, by_dst, g)
                    pe.wait_ge(hotT_done, g + 1)
                    at_least(pe, picked, g - 1)
                    for u in range(4):
                        at = u * R
                        last = pe.matmul(bank[4 + gq % 2][:, at:at + R], hotT[:, gq % 2, u * P:(u + 1) * P],
                                         rcnt[:, node_tile(ids[u], R)], start=True, stop=True)
                    last.then_inc(looked, 1)
                there, g, gi, gq = group(i, q, 2)
                if there:
                    pe.wait_ge(hot_w, g + 1)
                    at_least(pe, added1, 4 * (g - 1))
                    for u in range(4):
                        s = 4 * gq + u
                        pe.wait_ge(landed[s], 16 * (gi + 1))
                        last = pe.matmul(bank[2 * (gq % 2) + u // 2][:, (u % 2) * D:(u % 2 + 1) * D],
                                         hot[:, s % 8, :], rows[:, s, :], start=True, stop=True)
                    last.then_inc(summed1, 1)
                last = turn_hot(i, q, hot_ready, hotT_done)
                if last is not None:
                    last.then_inc(turnT, 1)
            turns(pe, step1, 3)

            turn_tiles(1, acc)
            products(1, w2_in)

            def step2(i, q):
                there, g, gi, gq = group(i, q, 1)
                if there:
                    pe.wait_ge(hot2, g + 1)
                    at_least(pe, added2, 4 * (g - 1))
                    for u in range(4):
                        s = 4 * gq + u
                        pe.wait_ge(landed[s], 16 * (gi + 1 + TURNS))
                        last = pe.matmul(bank[2 * (gq % 2) + u // 2][:, (u % 2) * D:(u % 2 + 1) * D],
                                         hot[:, s % 8, :], rows[:, s, :], start=True, stop=True)
                    last.then_inc(summed2, 1)
                there, g, gi, gq = group(i, q, 2)
                if there:
                    for u in range(4):
                        permute(4 * g + u + CHUNKS, 4 * (gq % 2) + u, isinstance(g, int) and g == 0 and u == 0, False)
            turns(pe, step2, 2)

            turn_tiles(2, acc)
            pe.wait_ge(wg_in, 48)
            pe.wait_ge(hT_done, 3 * TILES)
            for b in range(-(-TILES // 4)):
                w = min(512, TILES * P - b * 512)
                at_least(pe, x1_out, b - 1)
                for k in range(KH):
                    last = pe.matmul(bank[b % 2][0:OD, 0:w], wg_sb[:, k, :], hT[:, k, b * 512:b * 512 + w],
                                     start=(k == 0), stop=(k == KH - 1))
                last.then_inc(x1_prod, 1)
                pe.wait_ge(x1_out, b + 1)
                for j in range(w // P):
                    t = 4 * b + j
                    at_least(pe, tab_out, t - 1)
                    pe.matmul(bank[2 + t % 2][:, 0:TW + HEADS], x1T[:, j * P:(j + 1) * P], head_w[:, :],
                              start=True, stop=True).then_inc(tab_prod, 1)

            pe.wait_ge(tab_out, TILES)
            pe.wait_ge(order_done, 2)

            def step3(i, q):
                there, g, _, gq = group(i, q, 1)
                if there:
                    ids = tile_ids(PE, by_src, g)
                    pe.wait_ge(hotT3, g + 1)
                    at_least(pe, z_done, g - 1)
                    for u in range(4):
                        at = u * HEADS
                        last = pe.matmul(bank[4 + gq % 2][:, at:at + HEADS], hotT[:, gq % 2, u * P:(u + 1) * P],
                                         el_tab[:, node_tile(ids[u], HEADS)], start=True, stop=True)
                    last.then_inc(looked3, 1)
                there, g, gi, gq = group(i, q, 3)
                if there:
                    pe.wait_ge(rhs_done, g + 1)
                    pe.wait_ge(hot3_w, g + 1)
                    for u in range(4):
                        s = 4 * gq + u
                        at_least(pe, added3, 4 * (g - 1) + u + 1)
                        last = pe.matmul(bank[u][:, 0:AW], hot[:, s % 8, :], arhs[:, s % 8, :], start=True, stop=True)
                    last.then_inc(summed3, 1)
                last = turn_hot(i, q, hot3, hotT3)
                if last is not None:
                    last.then_inc(turnT3, 1)
            turns(pe, step3, 4)

        @block.scalar
        def _(act):
            def square_roots(n):
                act.wait_ge(normed_st, n + 1)
                act.activation(rstd[:, :], mv[:, :, 1], ACT.Sqrt, bias=eps_col[:, 0:1]).then_inc(sqrt_done, 1)

            def turned_out(phase):
                with act.Fori(0, TILES // 5) as i:
                    for u in range(5):
                        act.wait_ge(turned, (i * 5 + u + 1) + phase * TILES)
                        act.activation(hT[:, :, bass.ds((i * 5 + u) * P, P)],
                                       bank[u][:, 0:D].rearrange("p (k n) -> p k n", k=KH),
                                       ACT.Relu).then_inc(hT_done, 1)

            def y_pieces(layer):
                def pieces(t):
                    for n in range(YC):
                        act.wait_ge(y_prod, (t + layer * TILES) * YC + n + 1)
                        at_least(act, y_stored[n], 16 * (t + layer * TILES))
                        act.activation(ystage[:, n, :], bank[n][:, :], ACT.Copy).then_inc(y_out, 1)
                pieces(0)
                with act.Fori(1, TILES) as t:
                    pieces(t)

            def scale_lanes(c, u, o, used_before):
                act.wait_ge(perm_lane, used_before + c + 1)
                at_least(act, perm_used, used_before + c - RP + 1)
                act.activation(lanes_hi[:, u, :], lanes[:, u, :], ACT.Copy, scale=o.hi[:, bass.ds(c, 1)])
                act.activation(lanes_lo[:, u, :], lanes[:, u, :], ACT.Copy,
                               scale=o.lo[:, bass.ds(c, 1)]).then_inc(perm_scaled, 1)

            act.wait_ge(const_done, 1)
            square_roots(0)
            turned_out(0)
            y_pieces(0)

            act.wait_ge(hist_used, EC)
            for u in range(RP):
                scale_lanes(u, u, by_dst, 0)
            with act.Fori(1, CHUNKS // RP) as i:
                for u in range(RP):
                    scale_lanes(i * RP + u, u, by_dst, 0)

            def hot_turned(g, gq, turned_, looked_):
                act.wait_ge(turned_, g + 1)
                at_least(act, looked_, g - 1)
                return act.activation(hotT[:, gq % 2, :], turn16[gq % 2][:, 0:512], ACT.Copy)

            def step1(i, q):
                there, g, _, gq = group(i, q, 1)
                if there:
                    act.wait_ge(picked, g + 1)
                    at_least(act, summed1, g - 1)
                    for u in range(4):
                        s = 4 * gq + u
                        last = act.activation(hot[:, s % 8, :], hot16[:, s, :], ACT.Copy,
                                              scale=weight[:, bass.ds(4 * g + u, 1)])
                    last.then_inc(hot_w, 1)
                there, g, _, gq = group(i, q, 0)
                if there:
                    hot_turned(g, gq, turnT, looked).then_inc(hotT_done, 1)
            turns(act, step1, 1)

            turned_out(1)
            y_pieces(1)

            def step2(i, q):
                there, g, _, gq = group(i, q, 0)
                if there:
                    for u in range(4):
                        scale_lanes(4 * g + u, 4 * (gq % 2) + u, by_src, CHUNKS)
            turns(act, step2, 0)

            square_roots(1)
            turned_out(2)
            for b in range(-(-TILES // 4)):
                w = min(512, TILES * P - b * 512)
                act.wait_ge(x1_prod, b + 1)
                at_least(act, tab_prod, 4 * b)
                act.activation(x1T[:, 0:w], bank[b % 2][0:OD, 0:w], ACT.Copy).then_inc(x1_out, 1)

            def step3(i, q):
                there, g, _, gq = group(i, q, 1)
                if there:
                    act.wait_ge(z_done, g + 1)
                    at_least(act, summed3, g - 1)
                    act.activation(arhs[:, 4 * (gq % 2):4 * (gq % 2) + 4, D:AW], zbuf[:, gq % 2, :, :],
                                   ACT.Exp).then_inc(e_done, 1)
                    act.activation(hot[:, 4 * (gq % 2):4 * (gq % 2) + 4, :], hot16[:, 4 * gq:4 * gq + 4, :],
                                   ACT.Copy).then_inc(hot3_w, 1)
                there, g, _, gq = group(i, q, 0)
                if there:
                    hot_turned(g, gq, turnT3, looked3).then_inc(hotT3, 1)
            turns(act, step3, 1)

            for n in range(-(-TILES // 5)):
                act.wait_ge(low_done, n + 1)
                low = hT[:, 0, 0:5 * D] if n % 2 == 0 else hT[:, 1, 0:5 * D]
                act.activation(low, low, ACT.Exp).then_inc(exp_done, 1)

        @block.vector
        def _(dve):
            linked = [0]

            def link(ins):
                linked[0] += 1
                ins.then_inc(dve_link, 1)
                dve.wait_ge(dve_link, linked[0])

            def norm_tiles(n):
                with dve.Fori(0, TILES) as t:
                    dve.bn_stats(stats[:, bass.ds(t, 1), :].rearrange("p a b -> p (a b)"), xb[:, node_tile(t)])
                link(dve.drain())
                for t in range(TILES):
                    dve.bn_aggr(mv[:, t, :], stats[:, t, :])
                link(dve.drain())
                dve.nop().then_inc(normed_st, 1)
                dve.wait_ge(sqrt_done, n + 1)
                link(dve.reciprocal(rstd[:, :], rstd[:, :]))
                with dve.Fori(0, TILES) as t:
                    dve.tensor_scalar(acc[:, node_tile(t)], xb[:, node_tile(t)],
                                      mv[:, bass.ds(t, 1), 0:1].rearrange("p a b -> p (a b)"),
                                      rstd[:, bass.ds(t, 1)], ALU.subtract, ALU.mult).then_inc(normed, 1)

            def prepare(n, o, key, payload):
                real = slice(0, EC)
                link(dve.tensor_scalar(tmp_i[:, real], key, SHIFT, None, ALU.arith_shift_right))
                link(dve.tensor_scalar(low_i[:, real], key, P - 1, None, ALU.bitwise_and))
                link(dve.tensor_copy(tile_f[:, real], tmp_i[:, real]))
                if n == 0:
                    link(dve.tensor_copy(low_f[:, real], low_i[:, real]))
                    link(dve.scalar_tensor_tensor(out=key_f[:, real], in0=tile_f[:, real], scalar=float(R),
                                                  in1=et_i[:, :], op0=ALU.mult, op1=ALU.add))
                dve.nop().then_inc(counts_ready, 1)
                for k in range(TILES):
                    last = dve.tensor_scalar(member[:, k, :], tile_f[:, :], float(k), None, ALU.is_equal, ALU.add,
                                             accum_out=n_in[:, k:k + 1])
                link(dve.drain())
                dve.nop().then_inc(counts_ready, 1)
                dve.wait_ge(counts_summed, n + 1)
                link(dve.tensor_scalar(tot_i[:, :], small_ps[:, 0:TILES], float(P - 1), None, ALU.add))
                link(dve.tensor_scalar(tot_i[:, :], tot_i[:, :], SHIFT, None, ALU.arith_shift_right))
                link(dve.tensor_copy(nch[:, :], tot_i[:, :]))
                link(dve.tensor_tensor_scan(cend[:, :], nch[:, :], zeros[:, 0:TILES], 0.0, ALU.add, ALU.add))
                link(dve.tensor_tensor(start[:, :], cend[:, :], nch[:, :], ALU.subtract))
                link(dve.scalar_tensor_tensor(out=start[:, :], in0=start[:, :], scalar=float(P),
                                              in1=small_ps[:, TILES:2 * TILES], op0=ALU.mult, op1=ALU.add))
                link(dve.tensor_scalar(start[:, :], start[:, :], -1.0, None, ALU.add))
                dve.nop().then_inc(counts_read, 1)
                link(dve.memset(pos[:, :], -1.0))
                for k in range(TILES):
                    link(dve.tensor_tensor_scan(run[:, k % 2, :], member[:, k, :], zeros[0:EP, :],
                                                start[0:EP, k:k + 1], ALU.add, ALU.add))
                    link(dve.copy_predicated(pos[:, :], member[:, k, :], run[:, k % 2, :]))
                link(dve.tensor_copy(tmp_i[:, :], pos[:, :]))
                link(dve.tensor_scalar(tmp2_i[:, :], tmp_i[:, :], SHIFT, None, ALU.arith_shift_right))
                link(dve.tensor_copy(o.chunk[:, :], tmp2_i[:, :]))
                link(dve.tensor_scalar(tmp2_i[:, :], tmp_i[:, :], P - 1, None, ALU.bitwise_and))
                link(dve.tensor_copy(o.lane[:, :], tmp2_i[:, :]))
                row = payload()
                link(dve.tensor_scalar(tmp2_i[:, real], row, 4, None, ALU.arith_shift_right))
                link(dve.tensor_copy(o.hi[:, real], tmp2_i[:, real]))
                link(dve.tensor_scalar(tmp2_i[:, real], row, 15, None, ALU.bitwise_and))
                link(dve.scalar_tensor_tensor(out=o.lo[:, real], in0=tmp2_i[:, real], scalar=float(P),
                                              in1=low_i[:, real], op0=ALU.mult, op1=ALU.add))
                link(dve.tensor_scalar(o.lo[:, real], o.lo[:, real], 1.0, None, ALU.add))
                link(dve.memset(tid_f[:, :], 0.0))
                for k in range(TILES):
                    link(dve.scalar_tensor_tensor(out=tid_f[:, :], in0=iota16[0:1, 0:CHUNKS], scalar=cend[0:1, k:k + 1],
                                                  in1=tid_f[:, :], op0=ALU.is_ge, op1=ALU.add))
                link(dve.tensor_scalar(o.tid[:, :], tid_f[:, :], float(TILES - 1), None, ALU.min))

            def conv_row():
                link(dve.scalar_tensor_tensor(out=tmp_i[:, 0:EC], in0=src_i[:, :], scalar=float(R), in1=et_i[:, :],
                                              op0=ALU.mult, op1=ALU.add))
                return tmp_i[:, 0:EC]

            def roots(layer, bias, base, width):
                with dve.Fori(0, TILES // 5) as i:
                    for u in range(5):
                        t = i * 5 + u
                        dve.wait_ge(root_prod, t + 1 + layer * TILES)
                        if layer == 0:
                            dve.tensor_tensor(acc[:, node_tile(t)], bank[u][:, 0:D], bias[:, :],
                                              ALU.add).then_inc(root_added, 1)
                        else:
                            dve.tensor_tensor(xb[:, node_tile(t)], bank[u][:, 0:D], xb[:, node_tile(t)],
                                              ALU.add).then_inc(root_added, 1)

            def column(c, u, o, used_before):
                at_least(dve, perm_used, used_before + c - RP + 1)
                dve.tensor_scalar(wide[:, u, :], iota16[0:EP, 0:CHUNKS], o.chunk[:, bass.ds(c, 1)], None,
                                  ALU.is_equal).then_inc(perm_wide, 1)
                dve.tensor_scalar(lanes[:, u, :], iota16[0:EP, 0:P], o.lane[:, bass.ds(c, 1)], None,
                                  ALU.is_equal).then_inc(perm_lane, 1)

            def finish_order(o, n):
                dve.wait_ge(perm_used, CHUNKS * (n + 1))
                hi, lo = perm_ps[0][:, 0:CHUNKS], perm_ps[1][:, 0:CHUNKS]
                link(dve.tensor_scalar(slot_i[:, :], lo, -1.0, 0.0, ALU.add, ALU.max))
                link(dve.tensor_scalar(slot2_i[:, :], slot_i[:, :], SHIFT, None, ALU.arith_shift_right))
                link(dve.scalar_tensor_tensor(out=o.idx[:, :], in0=hi, scalar=16.0, in1=slot2_i[:, :],
                                              op0=ALU.mult, op1=ALU.add))
                link(dve.tensor_scalar(empty[:, :], lo, 0.0, None, ALU.is_equal))
                link(dve.tensor_scalar(slot2_i[:, :], slot_i[:, :], P - 1, None, ALU.bitwise_and))
                link(dve.scalar_tensor_tensor(out=o.loc[:, :], in0=empty[:, :], scalar=-float(P), in1=slot2_i[:, :],
                                              op0=ALU.mult, op1=ALU.add))
                if n == 0:
                    link(dve.tensor_scalar(slot2_i[:, :], o.idx[:, :], R - 1, None, ALU.bitwise_and))
                    link(dve.tensor_copy(et_f[:, :], slot2_i[:, :]))
                dve.nop().then_inc(order_done, 1)

            link(dve.memset(xb[:, (TILES - 1) * D:], 0.0))
            link(dve.memset(eps_col[:, :], EPS_LN))
            link(dve.memset(ones[:, :], 1.0))
            link(dve.memset(zeros[:, :], 0))
            link(dve.memset(tile_f[:, :], -1.0))
            for o in orders:
                link(dve.memset(o.hi[:, :], 0.0))
                link(dve.memset(o.lo[:, :], 0.0))
            dve.wait_ge(pool_const, 2)
            link(dve.tensor_scalar(ident[:, :], iota16[:, 0:P], lane_no[:, 0:1], None, ALU.is_equal))
            link(dve.tensor_scalar(ident16[:, :], iota16[:, 0:P], lane_no[:, 0:1], None, ALU.is_equal))
            link(dve.tensor_scalar(before[:, :], iota16[:, 0:P], lane_no[:, 0:1], None, ALU.is_gt))
            link(dve.tensor_scalar(head_w[:, 0:OD], iota16[0:OD, 0:OD], lane_no[0:OD, 0:1], None, ALU.is_equal))
            dve.nop().then_inc(const_done, 1)

            dve.wait_ge(x_in, 32)
            norm_tiles(0)
            dve.wait_ge(e_in, 48)
            prepare(0, by_dst, dst_i[:, :], conv_row)
            prepare(1, by_src, src_i[:, :], lambda: dst_i[:, :])
            dve.wait_ge(b_in, 48)
            dve.wait_ge(hT_done, TILES)
            roots(0, bias1, acc, D)

            def hist_keys(i):
                for u in range(RP):
                    at_least(dve, hist_used, (i - 1) * RP + u + 1)
                    dve.tensor_scalar(wide[:, u, 0:HC], iota16[0:EP, 0:HC], key_f[:, bass.ds(i * RP + u, 1)], None,
                                      ALU.is_equal).then_inc(hist_wide, 1)
            hist_keys(0)
            with dve.Fori(1, EC // RP) as i:
                hist_keys(i)
            dve.wait_ge(hist_used, EC)
            for u in range(RP):
                column(u, u, by_dst, 0)
            with dve.Fori(1, CHUNKS // RP) as i:
                for u in range(RP):
                    column(i * RP + u, u, by_dst, 0)
            link(dve.tensor_scalar(rcnt[:, :], hist_ps[:, 0:HC], 1.0, None, ALU.max))
            link(dve.reciprocal(rcnt[:, :], rcnt[:, :]))
            dve.nop().then_inc(rcnt_done, 1)
            finish_order(by_dst, 0)
            dve.wait_ge(root_added, TILES)

            def add_sums(i, q, lag, o, summed, added, target, width, where, already):
                there, g, _, gq = group(i, q, lag)
                if there:
                    ids = tile_ids(DVE, o, g)
                    dve.wait_ge(summed, g + 1)
                    for u in range(4):
                        at_least(dve, added, 4 * g + u)
                        sl = target[:, node_tile(ids[u], width)]
                        dve.tensor_tensor(sl, where(gq, u), sl, ALU.add).then_inc(added, 1)

            def conv_bank(gq, u):
                return bank[2 * (gq % 2) + u // 2][:, (u % 2) * D:(u % 2 + 1) * D]

            def step1(i, q):
                there, g, _, gq = group(i, q, 0)
                if there:
                    at_least(dve, hot_w, g - 3)
                    for u in range(4):
                        last = dve.tensor_scalar(hot16[:, 4 * gq + u, :], iota16[:, 0:P],
                                                 by_dst.loc[:, bass.ds(4 * g + u, 1)], None, ALU.is_equal)
                    last.then_inc(hot_ready, 1)
                there, g, _, gq = group(i, q, 1)
                if there:
                    dve.wait_ge(looked, g + 1)
                    at_least(dve, picked, g)
                    for u in range(4):
                        at = u * R
                        last = dve.scalar_tensor_tensor(out=trash[:, u, :], in0=iota16[:, 0:R],
                                                        scalar=et_f[:, bass.ds(4 * g + u, 1)],
                                                        in1=bank[4 + gq % 2][:, at:at + R], op0=ALU.is_equal, op1=ALU.mult,
                                                        accum_out=weight[:, bass.ds(4 * g + u, 1)])
                    last.then_inc(picked, 1)
                add_sums(i, q, 3, by_dst, summed1, added1, acc, D, conv_bank, 0)
            turns(dve, step1, 3)

            dve.wait_ge(added1, CHUNKS)
            with dve.Fori(0, TILES) as t:
                dve.tensor_tensor(xb[:, node_tile(t)], xb[:, node_tile(t)], bias2[:, :], ALU.add).then_inc(normed, 1)
            link(dve.drain())
            roots(1, bias2, xb, D)

            def step2(i, q):
                there, g, _, gq = group(i, q, 0)
                if there:
                    at_least(dve, summed2, g - 1)
                    for u in range(4):
                        c = 4 * g + u
                        last = dve.tensor_scalar(hot[:, 4 * (gq % 2) + u, :], iota16[:, 0:P],
                                                 by_dst.loc[:, bass.ds(c, 1)], weight[:, bass.ds(c, 1)],
                                                 ALU.is_equal, ALU.mult)
                    last.then_inc(hot2, 1)
                    for u in range(4):
                        column(4 * g + u, 4 * (gq % 2) + u, by_src, CHUNKS)
                add_sums(i, q, 2, by_dst, summed2, added2, xb, D, conv_bank, 0)
            dve.wait_ge(root_added, 2 * TILES)
            turns(dve, step2, 2)
            finish_order(by_src, 1)

            dve.wait_ge(added2, CHUNKS)
            norm_tiles(1)
            for t in range(TILES):
                dve.wait_ge(tab_prod, t + 1)
                dve.tensor_copy(tabst[:, t, :], bank[2 + t % 2][:, 0:TW])
                dve.tensor_copy(el_tab[:, t * HEADS:(t + 1) * HEADS],
                                bank[2 + t % 2][:, TW:TW + HEADS]).then_inc(tab_out, 1)
            dve.wait_ge(hT_done, 3 * TILES)
            link(dve.memset(acc[:, :], 0.0))

            def step3(i, q):
                there, g, _, gq = group(i, q, 0)
                if there:
                    at_least(dve, hot3_w, g - 3)
                    for u in range(4):
                        last = dve.tensor_scalar(hot16[:, 4 * gq + u, :], iota16[:, 0:P],
                                                 by_src.loc[:, bass.ds(4 * g + u, 1)], None, ALU.is_equal)
                    last.then_inc(hot3, 1)
                there, g, gi, gq = group(i, q, 1)
                if there:
                    for u in range(4):
                        dve.wait_ge(landed[4 * gq + u], 16 * (gi + 1 + 2 * TURNS))
                    dve.wait_ge(looked3, g + 1)
                    at_least(dve, e_done, g - 1)
                    dve.tensor_tensor(zbuf[:, gq % 2, :, :],
                                      bank[4 + gq % 2][:, 0:4 * HEADS].rearrange("p (u h) -> p u h", u=4),
                                      arows[:, 4 * gq:4 * gq + 4, OD:TW], ALU.add).then_inc(z_sum, 1)
                    dve.wait_ge(z_sum, g + 1)
                    zf = zbuf[:, gq % 2, :, :].rearrange("p u h -> p (u h)")
                    dve.scalar_tensor_tensor(out=zf, in0=zf, scalar=SLOPE, in1=zf, op0=ALU.mult,
                                             op1=ALU.max).then_inc(z_done, 1)
                add_sums(i, q, 4, by_src, summed3, added3, acc, AW, lambda gq, u: bank[u][:, 0:AW], 0)
                there, g, gi, gq = group(i, q, 2)
                if there:
                    dve.wait_ge(e_done, g + 1)
                    at_least(dve, summed3, g - 1)
                    for u in range(4):
                        s = 4 * gq + u
                        last = dve.tensor_tensor(
                            arhs[:, s % 8, 0:D].rearrange("p (h o) -> p h o", h=HEADS),
                            arows[:, s, 0:OD].unsqueeze(1).broadcast_to([P, HEADS, OD]),
                            arhs[:, s % 8, D:AW].unsqueeze(2).broadcast_to([P, HEADS, OD]), ALU.mult)
                    last.then_inc(rhs_done, 1)
            turns(dve, step3, 4)

            dve.wait_ge(added3, CHUNKS)
            av = acc[:, :].rearrange("p (t c) -> p t c", c=AW)
            rsum = tabst[:, :, 0:HEADS]
            dve.wait_ge(tab_stored, 16)
            link(dve.tensor_scalar(rsum, av[:, :, D:AW], EPS_ROW, None, ALU.max))
            link(dve.reciprocal(rsum, rsum))
            for n in range(-(-TILES // 5)):
                low = hT[:, n % 2, 0:5 * D]
                for t in range(5 * n, 5 * n + 5):
                    v = av[:, t, 0:D].rearrange("p (h o) -> p h o", h=HEADS)
                    link(dve.tensor_tensor(v, v, rsum[:, t, :].unsqueeze(2).broadcast_to([P, HEADS, OD]), ALU.mult))
                    link(dve.tensor_tensor(v, v, biasg[:, :].unsqueeze(1).broadcast_to([P, HEADS, OD]), ALU.add))
                v5 = av[:, 5 * n:5 * n + 5, 0:D]
                link(dve.tensor_scalar(low.rearrange("p (t d) -> p t d", t=5), v5, 0.0, None, ALU.min))
                dve.nop().then_inc(low_done, 1)
                dve.wait_ge(exp_done, n + 1)
                link(dve.scalar_tensor_tensor(out=low.rearrange("p (t d) -> p t d", t=5), in0=v5, scalar=0.0,
                                              in1=low.rearrange("p (t d) -> p t d", t=5), op0=ALU.max, op1=ALU.add))
                xs = xb[:, 5 * n * D:5 * (n + 1) * D]
                link(dve.scalar_tensor_tensor(out=xs, in0=low, scalar=-1.0, in1=xs, op0=ALU.add, op1=ALU.add))
                dve.nop().then_inc(out_done, 1)


_INS = ["x", "src", "dst", "edge_type_8", "L0_gnn_W1", "L0_gnn_Wroot1", "L0_gnn_b1", "L0_gnn_W2", "L0_gnn_Wroot2",
        "L0_gnn_b2", "L1_gnn_W", "L1_gnn_Wl", "L1_gnn_Wr", "L1_gnn_b"]


def kernel(**inputs):
    import concourse.bacc as bacc
    from concourse.bass_utils import run_bass_kernel_spmd

    nc = bacc.Bacc("TRN2", target_bir_lowering=False, num_devices=1)
    arrays, args = {}, []
    for name in _INS:
        a = np.ascontiguousarray(inputs[name])
        arrays[f"in_{name}"] = a
        args.append(nc.dram_tensor(f"in_{name}", a.shape, mybir.dt.from_np(a.dtype), kind="ExternalInput").ap())
    shape = inputs["x"].shape
    args.append(nc.dram_tensor("out_0", shape, F32, kind="ExternalOutput").ap())
    build_gnn(nc, *args)
    r = run_bass_kernel_spmd(nc, [arrays], core_ids=[0])
    return r.results[0]["out_0"]
```

```python
from contextlib import ExitStack

import numpy as np

import concourse.bass as bass
from concourse import mybir

F32 = mybir.dt.float32
F16 = mybir.dt.float16
I32 = mybir.dt.int32
U8 = mybir.dt.uint8
ALU = mybir.AluOpType
ACT = mybir.ActivationFunctionType
PE = mybir.EngineType.PE
DVE = mybir.EngineType.DVE

P = 128
SHIFT = 7


def build_gnn(nc, x, src, dst, etype, W1, Wroot1, b1, W2, Wroot2, b2, Wg, Wl, Wr, bg, out):
    N, D = x.shape
    E = src.shape[0]
    R = W1.shape[0]
    OD, HEADS = Wg.shape[1], Wl.shape[0]
    TILES = -(-N // P)
    TAIL = N - (TILES - 1) * P
    KH = D // P
    EP = next(p for p in range(P, 0, -1) if E % p == 0)
    EC = E // EP
    CHUNKS = -(-(E // P + TILES) // 16) * 16
    GROUPS = CHUNKS // 4
    TURNS = GROUPS // 4
    PLAIN_TURNS = 3
    HIST_IN_TURNS = (TILES // 5 - PLAIN_TURNS) * 40
    assert TILES % 5 == 0 and GROUPS % 8 == 0 and EC % 16 == 0
    assert CHUNKS >= EC and CHUNKS >= E // P + TILES and CHUNKS <= 512
    assert KH == 2 and HEADS * OD == D
    YC = R * D // 512
    HC = TILES * R
    TW = OD + HEADS
    AW = D + HEADS
    EPS_LN, EPS_ROW, SLOPE = 1e-5, 1e-12, 0.2

    y_dram = nc.dram_tensor("y_rows", (TILES * P * R, D), F32, kind="Internal").ap()
    tab_dram = nc.dram_tensor("attention_rows", (TILES * P, TW), F32, kind="Internal").ap()
    y_tiles = y_dram.rearrange("(t p r) d -> p t (r d)", p=P, r=R)
    tab_tiles = tab_dram.rearrange("(t p) c -> p t c", p=P)

    with ExitStack() as ctx:
        def sb(name, shape, dt):
            return ctx.enter_context(nc.sbuf_tensor(name, shape, dt))

        def sem(name):
            return ctx.enter_context(nc.semaphore(name))

        bank = [ctx.enter_context(nc.psum_tensor(f"bank{i}", [P, 512], F32)) for i in range(6)]
        turn16 = [ctx.enter_context(nc.psum_tensor(f"turn16_{i}", [P, 1024], F16)) for i in range(2)]
        root_ps, turn_ps, count_ps, hist_ps = bank[2:6]
        perm_ps = [t[:, :].bitcast(F32) for t in turn16]

        iota16 = sb("iota16", [P, 512], F16)
        iota4 = sb("iota4", [P, P, 4], F16)
        lane_no = sb("lane_no", [P, 1], F32)
        ident = sb("ident", [P, P], F32)
        ident16 = sb("ident16", [P, P], F16)
        before = sb("before", [P, P], F32)
        ones = sb("ones", [P, P], F32)
        zeros16 = sb("zeros16", [P, CHUNKS], F16)
        eps_col = sb("eps_col", [P, 1], F32)
        bias1 = sb("bias1", [P, D], F32)
        bias2 = sb("bias2", [P, D], F32)
        biasg = sb("biasg", [P, OD], F32)

        xb = sb("xb", [P, TILES * D], F32)
        acc = sb("acc", [P, TILES * AW], F32)
        feed = sb("feed", [P, 5, D], F32)
        hT = sb("hT", [P, 5, D], F32)
        w_sb = sb("w_sb", [P, KH, R * D], F32)
        wroot_sb = sb("wroot_sb", [P, KH, D], F32)
        stats = sb("stats", [P, TILES, 6], F32)
        mv = sb("mv", [P, TILES, 2], F32)
        rstd = sb("rstd", [P, TILES], F32)
        rcnt = sb("rcnt", [P, HC], F32)
        wg_sb = sb("wg_sb", [P, KH, OD], F32)
        head_w = sb("head_w", [OD, OD + 2 * HEADS], F32)
        x1T = sb("x1T", [OD, 5, P], F32)
        tabst = sb("tabst", [P, TILES, TW], F32)
        el_tab = sb("el_tab", [P, TILES * HEADS], F32)

        src_i = sb("src_i", [EP, EC], I32)
        dst_i = sb("dst_i", [EP, EC], I32)
        et_i = sb("et_i", [EP, EC], I32)
        lists = sb("lists", [EP, 9, CHUNKS], F32)
        tmp_i, tmp2_i, low_i = (lists[:, k, :].bitcast(I32) for k in range(3))
        tile_f, pos, tile_rel = (lists[:, k, :] for k in range(3, 6))
        run = lists[:, 6:8, :]
        low16 = lists[:, 8, 0:CHUNKS // 2].bitcast(F16)
        n_in = sb("n_in", [EP, TILES], F32)
        tot_i = sb("tot_i", [P, TILES], I32)
        nch = sb("nch", [P, TILES], F32)
        cend = sb("cend", [P, TILES], F32)
        start = sb("start", [P, TILES], F32)
        tid_f = sb("tid_f", [1, CHUNKS], F32)

        class Order:
            pass
        orders = []
        for name in ("dst", "src"):
            o = Order()
            o.chunk = sb(f"{name}_chunk", [EP, CHUNKS], F32)
            o.lane = sb(f"{name}_lane", [EP, CHUNKS], F16)
            o.hi = sb(f"{name}_hi", [EP, CHUNKS], F32)
            o.lo = sb(f"{name}_lo", [EP, CHUNKS], F16)
            o.tid = sb(f"{name}_tid", [1, CHUNKS], I32)
            o.idx = sb(f"{name}_idx", [P, CHUNKS + 4], I32)
            o.loc = sb(f"{name}_loc", [P, CHUNKS], F32)
            orders.append(o)
        by_dst, by_src = orders
        et_f = sb("et_f", [P, CHUNKS], F32)
        weight = sb("weight", [P, CHUNKS], F32)
        slot_i = sb("slot_i", [P, CHUNKS], I32)
        slot2_i = sb("slot2_i", [P, CHUNKS], I32)
        empty = sb("empty", [P, CHUNKS], F32)

        cols = sb("cols", [P, 8 * CHUNKS + 3 * 8 * P], F32)
        wide = cols[0:EP, 0:8 * CHUNKS].bitcast(F16).rearrange("p (s c) -> p s c", c=CHUNKS)
        lanes, lanes_hi, lanes_lo = (cols[0:EP, 8 * (CHUNKS + k * P):8 * (CHUNKS + (k + 1) * P)].bitcast(F16)
                                     .rearrange("p (b l u) -> p b l u", b=4, u=4) for k in range(3))
        for n, o in enumerate(orders):
            o.member = cols[0:EP, n * TILES * CHUNKS // 4:(n + 1) * TILES * CHUNKS // 4].bitcast(U8).rearrange(
                "p (k c) -> p k c", c=CHUNKS)
        arhs = cols[:, 0:16 * AW].rearrange("p (s c) -> p s c", c=AW)
        arows = cols[:, 16 * AW:16 * (AW + TW)].rearrange("p (s c) -> p s c", c=TW)
        rows = sb("rows", [P, 16, D], F32)
        ystage = rows[:, :, :].rearrange("p s d -> p (s d)").rearrange("p (n w) -> p n w", w=512)
        idx_ring = sb("idx_ring", [P, 32], I32)
        hot = sb("hot", [P, 16, P], F32)
        hots = sb("hots", [P, 16 * P], F32)
        hot16 = hots[:, 0:8 * P].bitcast(F16).rearrange("p (s n) -> p s n", n=P)
        hotT = hots[:, 8 * P:16 * P].rearrange("p (a n) -> p a n", a=2)
        zbuf = sb("zbuf", [P, 4, 4, HEADS], F32)
        trash = sb("trash", [P, 4, R], F32)
        expo = rows[:, :, :].rearrange("p s d -> p (s d)")

        x_in, e_in, b_in = sem("x_in"), sem("e_in"), sem("b_in")
        w1_in, w2_in, wg_in = sem("w1_in"), sem("w2_in"), sem("wg_in")
        pool_const, const_done = sem("pool_const"), sem("const_done")
        dve_link = sem("dve_link")
        stats_done, sqrt_done = sem("stats_done"), sem("sqrt_done")
        normed = sem("normed")
        fed, turned, hT_done = sem("fed"), sem("turned"), sem("hT_done")
        y_prod = sem("y_prod")
        y_out = sem("y_out")
        y_stored = [sem(f"y_stored{n}") for n in range(YC)]
        root_prod, root_out = sem("root_prod"), sem("root_out")
        counts_ready = sem("counts_ready")
        counts_summed, counts_read = sem("counts_summed"), sem("counts_read")
        hist_ready, hist_used = sem("hist_ready"), sem("hist_used")
        rcnt_done = sem("rcnt_done")
        perm_lane, perm_ready = sem("perm_lane"), sem("perm_ready")
        perm_hi, perm_used = sem("perm_hi"), sem("perm_used")
        order_done = sem("order_done")
        idx_placed, pool_passed = sem("idx_placed"), sem("pool_passed")
        landed = [sem(f"landed{s}") for s in range(16)]
        hot_ready, turnT, hotT_done = sem("hot_ready"), sem("turnT"), sem("hotT_done")
        looked, picked, hot_w = sem("looked"), sem("picked"), sem("hot_w")
        summed1, added1 = sem("summed1"), sem("added1")
        hot2, summed2, added2 = sem("hot2"), sem("summed2"), sem("added2")
        x1_prod, x1_out, tab_prod, tab_out = sem("x1_prod"), sem("x1_out"), sem("tab_prod"), sem("tab_out")
        tab_stored = sem("tab_stored")
        hot3, turnT3, hotT3, looked3 = sem("hot3"), sem("turnT3"), sem("hotT3"), sem("looked3")
        z_sum, z_done, e_done, rhs_done = sem("z_sum"), sem("z_done"), sem("e_done"), sem("rhs_done")
        hot3_w, summed3, added3 = sem("hot3_w"), sem("summed3"), sem("added3")
        value_done, below, plus_done = sem("value_done"), sem("below"), sem("plus_done")
        exp_done, out_done, out_stored = sem("exp_done"), sem("out_done"), sem("out_stored")

        def at_least(eng, s, value):
            if not (isinstance(value, int) and value <= 0):
                eng.wait_ge(s, value)

        def turns(eng, step, lag, count=GROUPS, ring=4, peel=0):
            first = peel or (2 if lag >= 2 else 1)
            for i in range(first):
                for q in range(ring):
                    step(i, q)
            with eng.Fori(first, count // ring) as i:
                for q in range(ring):
                    step(i, q)
            for q in range(lag):
                step(count // ring, q)

        def item(i, q, lag, count=GROUPS, ring=4):
            i2, q2 = i + (q - lag) // ring, (q - lag) % ring
            there = not isinstance(i, int) or 0 <= ring * i2 + q2 < count
            return there, ring * i2 + q2, i2, q2

        def tile_ids(engine, o, g):
            _, ids = nc.values_load_multi_w_load_instructions(
                o.tid[0:1, bass.ds(4 * g, 4)], engines=[engine], min_val=0, max_val=TILES - 1,
                skip_runtime_bounds_check_because="the ids are clamped to TILES - 1 when they are made")
            return ids

        def node_tile(t, width=D):
            return bass.ds(t * width, width)

        block = ctx.enter_context(nc.Block())

        @block.sync
        def _(sp):
            sp.dma_start(dst_i[:, :], dst.rearrange("(p c) -> p c", p=EP)).then_inc(e_in, 16)
            sp.dma_start(src_i[:, :], src.rearrange("(p c) -> p c", p=EP)).then_inc(e_in, 16)
            sp.dma_start(et_i[:, :], etype.rearrange("(p c) -> p c", p=EP)).then_inc(e_in, 16)
            sp.wait_ge(const_done, 1)
            sp.dma_start(xb[:, 0:(TILES - 1) * D].rearrange("p (t d) -> p t d", d=D),
                         x[0:(TILES - 1) * P, :].rearrange("(t p) d -> p t d", p=P)).then_inc(x_in, 16)
            sp.dma_start(xb[0:TAIL, (TILES - 1) * D:], x[(TILES - 1) * P:, :]).then_inc(x_in, 16)

            def load_weights(W, Wroot, done):
                for k in range(KH):
                    sp.dma_start(w_sb[:, k, :].rearrange("p (r e) -> p r e", r=R),
                                 W[:, k * P:(k + 1) * P, :].rearrange("r p e -> p r e")).then_inc(done, 16)
                sp.dma_start(wroot_sb[:, :, :], Wroot.rearrange("(k p) e -> p k e", p=P)).then_inc(done, 16)

            load_weights(W1, Wroot1, w1_in)
            sp.dma_start(bias1[:, :], b1.unsqueeze(0).broadcast_to([P, D])).then_inc(b_in, 16)
            sp.dma_start(bias2[:, :], b2.unsqueeze(0).broadcast_to([P, D])).then_inc(b_in, 16)
            sp.dma_start(biasg[:, :], bg.unsqueeze(0).broadcast_to([P, OD])).then_inc(b_in, 16)
            sp.dma_start(wg_sb[:, :, :], Wg.rearrange("(k p) e -> p k e", p=P)).then_inc(wg_in, 16)
            with nc.allow_non_contiguous_dma(reason="two 64 x 4 matrices, turned"):
                sp.dma_start(head_w[:, OD:OD + HEADS], Wr.rearrange("h o -> o h")).then_inc(wg_in, 16)
                sp.dma_start(head_w[:, OD + HEADS:], Wl.rearrange("h o -> o h")).then_inc(wg_in, 16)

            def store_y(layer):
                with sp.Fori(0, TILES) as t:
                    for n in range(YC):
                        sp.wait_ge(y_out, (t + layer * TILES) * YC + n + 1)
                        sp.dma_start(y_tiles[:, bass.ds(t, 1), n * 512:(n + 1) * 512],
                                     ystage[:, n:n + 1, :]).then_inc(y_stored[n], 16)

            store_y(0)
            sp.wait_ge(root_prod, TILES)
            load_weights(W2, Wroot2, w2_in)
            sp.wait_ge(added1, CHUNKS)
            store_y(1)

            for n in range(5):
                sp.wait_ge(tab_out, (n + 1) * TILES // 5)
                part = slice(n * TILES // 5, (n + 1) * TILES // 5)
                sp.dma_start(tab_tiles[:, part, :], tabst[:, part, :]).then_inc(tab_stored, 16)

            for t in range(0, TILES, 5):
                sp.wait_ge(out_done, t // 5 + 1)
                last = t + 5 >= TILES
                full = TILES - 1 - t if last else 5
                sp.dma_start(out[t * P:(t + full) * P, :].rearrange("(t p) d -> p t d", p=P),
                             xb[:, t * D:(t + full) * D].rearrange("p (t d) -> p t d", d=D)).then_inc(out_stored, 16)
                if last:
                    sp.dma_start(out[(TILES - 1) * P:, :], xb[0:TAIL, (TILES - 1) * D:]).then_inc(out_stored, 16)
            sp.wait_ge(out_stored, 16 * (-(-TILES // 5) + 1))

        @block.gpsimd
        def _(pool):
            pool.iota(iota16[:, :], [[1, 512]], base=0, channel_multiplier=0,
                      allow_small_or_imprecise_dtypes=True).then_inc(pool_const, 1)
            pool.iota(iota4[:, :, :], [[1, P], [0, 4]], base=0, channel_multiplier=0,
                      allow_small_or_imprecise_dtypes=True).then_inc(pool_const, 1)
            pool.iota(lane_no[:, :], [[1, 1]], base=0, channel_multiplier=1,
                      allow_small_or_imprecise_dtypes=True).then_inc(pool_const, 1)

            def feed_tiles(phase):
                def step(i, q):
                    t = 5 * i + q
                    if phase != 1:
                        pool.wait_ge(normed, t + 1 + phase // 2 * TILES)
                    at_least(pool, turned, t - 4 + phase * TILES)
                    pool.tensor_copy(feed[:, q, :], acc[:, node_tile(t)]).then_inc(fed, 1)
                turns(pool, step, 0, TILES, 5)

            def gather(layer, o, table, ring, used):
                def place(q, g):
                    pool.tensor_copy(idx_ring[:, 4 * q:4 * q + 4], o.idx[:, bass.ds(4 * g, 4)]).then_inc(idx_placed, 1)

                def step(i, q):
                    g = 8 * i + q
                    at_least(pool, used, g - 3)
                    pool.wait_ge(idx_placed, g + 1 + layer * (GROUPS + 1))
                    pool.sem_inc(pool_passed, 1)
                    for u in range(4):
                        if u == 2:
                            place((q + 1) % 8, g + 1)
                        s = 4 * (q % 4) + u
                        pool.indirect_dma_start(
                            out=ring[:, s, :], out_offset=None, in_=table,
                            in_offset=bass.IndirectOffsetOnAxis(ap=idx_ring[:, 4 * q + u:4 * q + u + 1], axis=0),
                        ).then_inc(landed[s], 16)
                place(0, 0)
                turns(pool, step, 0, GROUPS, 8)

            feed_tiles(0)
            pool.wait_ge(order_done, 1)
            for n in range(YC):
                pool.wait_ge(y_stored[n], 16 * TILES)
            gather(0, by_dst, y_dram, rows, summed1)
            pool.wait_ge(added1, CHUNKS)
            feed_tiles(1)
            for n in range(YC):
                pool.wait_ge(y_stored[n], 32 * TILES)
            gather(1, by_dst, y_dram, rows, summed2)
            feed_tiles(2)
            pool.wait_ge(order_done, 2)
            pool.wait_ge(tab_stored, 80)
            gather(2, by_src, tab_dram, arows, rhs_done)

            for n in range(5):
                pool.wait_ge(plus_done, n + 1)
                xs = xb[:, 5 * n * D:5 * (n + 1) * D]
                pool.tensor_tensor(xs, xs, expo[:, (n % 2) * 5 * D:(n % 2 + 1) * 5 * D], ALU.add).then_inc(out_done, 1)

        @block.tensor
        def _(pe):
            def turn_tile(i, q, phase):
                there, t, _, tq = item(i, q, 0, TILES, 5)
                if there:
                    pe.wait_ge(fed, t + 1 + phase * TILES)
                    at_least(pe, hT_done, t + phase * TILES)
                    for k in range(KH):
                        last = pe.transpose(turn_ps[:, k * P:(k + 1) * P], feed[:, tq, k * P:(k + 1) * P], ident[:, :])
                    last.then_inc(turned, 1)

            def product_tile(i, q, layer):
                there, t, _, tq = item(i, q, 1, TILES, 5)
                if there:
                    pe.wait_ge(hT_done, t + 1 + layer * TILES)
                    for n in range(YC):
                        at_least(pe, y_out, (t + layer * TILES) * YC + n - 1)
                        for k in range(KH):
                            last = pe.matmul(bank[n % 2][:, :], hT[:, tq, k * P:(k + 1) * P],
                                             w_sb[:, k, n * 512:(n + 1) * 512], start=(k == 0), stop=(k == KH - 1))
                        last.then_inc(y_prod, 1)
                    at_least(pe, root_out, t + layer * TILES)
                    for k in range(KH):
                        last = pe.matmul(root_ps[:, 0:D], hT[:, tq, k * P:(k + 1) * P], wroot_sb[:, k, :],
                                         start=(k == 0), stop=(k == KH - 1))
                    last.then_inc(root_prod, 1)

            def histogram(c4, b):
                pe.wait_ge(hist_ready, c4 + 1)
                for u in range(4):
                    last = pe.matmul(hist_ps[:, 0:HC], lanes[:, b, :, u], wide[:, 4 * b + u, 0:HC],
                                     start=False, stop=False, skip_group_check=True)
                last.then_inc(hist_used, 1)

            def permute(c4, b):
                pe.wait_ge(perm_ready, c4 + 1)
                pe.wait_ge(perm_hi, c4 + 1)
                for u in range(4):
                    pe.matmul(perm_ps[0][:, 0:CHUNKS], lanes_hi[:, b, :, u], wide[:, 4 * b + u, :],
                              start=False, stop=False, skip_group_check=True)
                    last = pe.matmul(perm_ps[1][:, 0:CHUNKS], lanes_lo[:, b, :, u], wide[:, 4 * b + u, :],
                                     start=False, stop=False, skip_group_check=True)
                last.then_inc(perm_used, 1)

            def open_sum(ps, width):
                pe.matmul(ps[:, 0:width], zeros16[:, 0:P], zeros16[:, 0:width], start=True, stop=False,
                          skip_group_check=True)

            def sum_counts(n):
                pe.wait_ge(counts_ready, n + 1)
                at_least(pe, counts_read, n)
                pe.matmul(count_ps[:, 0:TILES], ones[0:EP, :], n_in[:, :], start=True, stop=True)
                pe.matmul(count_ps[:, TILES:2 * TILES], before[0:EP, :], n_in[:, :],
                          start=True, stop=True).then_inc(counts_summed, 1)

            pe.wait_ge(const_done, 1)
            sum_counts(0)
            pe.wait_ge(w1_in, 16 * (KH + 1))

            def layer1(i, q):
                turn_tile(i, q, 0)
                product_tile(i, q, 0)

            for q in range(5):
                layer1(0, q)
            sum_counts(1)
            with pe.Fori(1, PLAIN_TURNS) as i:
                for q in range(5):
                    layer1(i, q)
            open_sum(hist_ps, HC)
            with pe.Fori(PLAIN_TURNS, TILES // 5) as i:
                for q in range(5):
                    layer1(i, q)
                    for k in range(8):
                        histogram((i - PLAIN_TURNS) * 40 + q * 8 + k, (q * 8 + k) % 4)
            layer1(TILES // 5, 0)
            with pe.Fori(HIST_IN_TURNS // 4, EC // 16) as i:
                for b in range(4):
                    histogram(4 * i + b, b)

            open_sum(perm_ps[0], CHUNKS)
            open_sum(perm_ps[1], CHUNKS)
            with pe.Fori(0, GROUPS // 4) as i:
                for b in range(4):
                    permute(4 * i + b, b)

            pe.wait_ge(rcnt_done, 1)
            pe.wait_ge(order_done, 1)

            def turn_hot(g, gq, ready, read_out, done):
                pe.wait_ge(ready, g + 1)
                at_least(pe, read_out, g - 1)
                for u in range(4):
                    last = pe.transpose(turn16[gq % 2][:, u * P:(u + 1) * P], hot16[:, 4 * gq + u, :], ident16[:, :])
                last.then_inc(done, 1)

            def look_up(g, gq, ids, table, width, ready, used, done):
                pe.wait_ge(ready, g + 1)
                at_least(pe, used, g - 1)
                for u in range(4):
                    last = pe.matmul(bank[4 + gq % 2][:, u * width:(u + 1) * width],
                                     hotT[:, gq % 2, u * P:(u + 1) * P], table[:, node_tile(ids[u], width)],
                                     start=True, stop=True)
                last.then_inc(done, 1)

            def sum_rows(g, gi, gq, layer, ready, added, done):
                pe.wait_ge(ready, g + 1)
                at_least(pe, added, 4 * (g - 1))
                for u in range(4):
                    s = 4 * gq + u
                    pe.wait_ge(landed[s], 16 * (gi + 1 + layer * TURNS))
                    last = pe.matmul(bank[2 * (gq % 2) + u // 2][:, (u % 2) * D:(u % 2 + 1) * D],
                                     hot[:, s, :], rows[:, s, :], start=True, stop=True)
                last.then_inc(done, 1)

            def step1(i, q):
                there, g, _, gq = item(i, q, 0)
                if there:
                    turn_hot(g, gq, hot_ready, hotT_done, turnT)
                there, g, _, gq = item(i, q, 1)
                if there:
                    look_up(g, gq, tile_ids(PE, by_dst, g), rcnt, R, hotT_done, picked, looked)
                there, g, gi, gq = item(i, q, 3)
                if there:
                    sum_rows(g, gi, gq, 0, hot_w, added1, summed1)
            turns(pe, step1, 3)

            pe.wait_ge(w2_in, 16 * (KH + 1))

            def layer2(i, q):
                turn_tile(i, q, 1)
                product_tile(i, q, 1)
            turns(pe, layer2, 1, TILES, 5)

            open_sum(perm_ps[0], CHUNKS)
            open_sum(perm_ps[1], CHUNKS)

            def step2(i, q):
                there, g, gi, gq = item(i, q, 1)
                if there:
                    sum_rows(g, gi, gq, 1, hot2, added2, summed2)
                    permute(g + GROUPS, gq)
            turns(pe, step2, 1)

            pe.wait_ge(wg_in, 48)

            def table_rows(i, q):
                turn_tile(i, q, 2)
                there, t, _, tq = item(i, q, 1, TILES, 5)
                if there:
                    pe.wait_ge(hT_done, t + 1 + 2 * TILES)
                    at_least(pe, x1_out, t)
                    for k in range(KH):
                        last = pe.matmul(bank[0][0:OD, 0:P], wg_sb[:, k, :], hT[:, tq, k * P:(k + 1) * P],
                                         start=(k == 0), stop=(k == KH - 1))
                    last.then_inc(x1_prod, 1)
                there, t, _, tq = item(i, q, 2, TILES, 5)
                if there:
                    pe.wait_ge(x1_out, t + 1)
                    at_least(pe, tab_out, t)
                    pe.matmul(bank[1][:, 0:TW + HEADS], x1T[:, tq, :], head_w[:, :],
                              start=True, stop=True).then_inc(tab_prod, 1)
            turns(pe, table_rows, 2, TILES, 5)

            pe.wait_ge(tab_out, TILES)
            pe.wait_ge(order_done, 2)

            def step3(i, q):
                there, g, gi, gq = item(i, q, 4)
                if there:
                    pe.wait_ge(rhs_done, g + 1)
                    pe.wait_ge(hot3_w, g + 1)
                    for u in range(4):
                        s = 4 * gq + u
                        at_least(pe, added3, 4 * (g - 1) + u + 1)
                        last = pe.matmul(bank[u][:, 0:AW], hot[:, s, :], arhs[:, s, :], start=True, stop=True)
                        last.then_inc(summed3, 1)
                there, g, _, gq = item(i, q, 1)
                if there:
                    look_up(g, gq, tile_ids(PE, by_src, g), el_tab, HEADS, hotT3, z_done, looked3)
                there, g, _, gq = item(i, q, 0)
                if there:
                    turn_hot(g, gq, hot3, hotT3, turnT3)
            turns(pe, step3, 4)

        @block.scalar
        def _(act):
            def square_roots(n):
                act.wait_ge(stats_done, n + 1)
                act.activation(rstd[:, :], mv[:, :, 1], ACT.Sqrt, bias=eps_col[:, 0:1]).then_inc(sqrt_done, 1)

            def turned_out(i, q, phase):
                there, t, _, tq = item(i, q, 0, TILES, 5)
                if there:
                    act.wait_ge(turned, t + 1 + phase * TILES)
                    if phase < 2:
                        at_least(act, root_prod, t - 4 + phase * TILES)
                    else:
                        at_least(act, x1_prod, t - 4)
                    act.activation(hT[:, tq, :], turn_ps[:, 0:D], ACT.Relu).then_inc(hT_done, 1)

            def pieces_out(i, q, layer):
                there, t, _, tq = item(i, q, 1, TILES, 5)
                if there:
                    for n in range(YC):
                        act.wait_ge(y_prod, (t + layer * TILES) * YC + n + 1)
                        at_least(act, y_stored[n], 16 * (t + layer * TILES))
                        act.activation(ystage[:, n, :], bank[n % 2][:, :], ACT.Copy).then_inc(y_out, 1)
                    if layer == 0:
                        act.wait_ge(root_prod, t + 1)
                        act.activation(acc[:, node_tile(t)], root_ps[:, 0:D], ACT.Copy).then_inc(root_out, 1)

            def high_lanes(g, b, o, before_):
                act.wait_ge(perm_lane, g + before_ + 1)
                for u in range(4):
                    last = act.activation(lanes_hi[:, b, :, u], lanes[:, b, :, u], ACT.Copy,
                                          scale=o.hi[:, bass.ds(4 * g + u, 1)])
                last.then_inc(perm_hi, 1)

            act.wait_ge(const_done, 1)
            square_roots(0)

            def layer1(i, q):
                turned_out(i, q, 0)
                pieces_out(i, q, 0)
            turns(act, layer1, 1, TILES, 5)
            turns(act, lambda i, q: high_lanes(4 * i + q, q, by_dst, 0), 0)

            def hot_turned(g, gq, turned_, used):
                act.wait_ge(turned_, g + 1)
                at_least(act, used, g - 1)
                return act.activation(hotT[:, gq % 2, :], turn16[gq % 2][:, 0:512], ACT.Copy)

            def step1(i, q):
                there, g, _, gq = item(i, q, 0)
                if there:
                    hot_turned(g, gq, turnT, looked).then_inc(hotT_done, 1)
                there, g, _, gq = item(i, q, 2)
                if there:
                    act.wait_ge(picked, g + 1)
                    at_least(act, summed1, g - 3)
                    for u in range(4):
                        last = act.activation(hot[:, 4 * gq + u, :], hot16[:, 4 * gq + u, :], ACT.Copy,
                                              scale=weight[:, bass.ds(4 * g + u, 1)])
                    last.then_inc(hot_w, 1)
            turns(act, step1, 2)

            def layer2(i, q):
                turned_out(i, q, 1)
                pieces_out(i, q, 1)
            turns(act, layer2, 1, TILES, 5)
            turns(act, lambda i, q: high_lanes(4 * i + q, q, by_src, GROUPS), 0)

            square_roots(1)

            def table_rows(i, q):
                turned_out(i, q, 2)
                there, t, _, tq = item(i, q, 1, TILES, 5)
                if there:
                    act.wait_ge(x1_prod, t + 1)
                    at_least(act, tab_prod, t - 4)
                    act.activation(x1T[:, tq, :], bank[0][0:OD, 0:P], ACT.Copy).then_inc(x1_out, 1)
            turns(act, table_rows, 1, TILES, 5, 2)

            def step3(i, q):
                there, g, _, gq = item(i, q, 2)
                if there:
                    act.wait_ge(z_done, g + 1)
                    at_least(act, summed3, 4 * (g - 3))
                    act.activation(arhs[:, 4 * gq:4 * gq + 4, D:AW], zbuf[:, gq, :, :], ACT.Exp).then_inc(e_done, 1)
                    act.activation(hot[:, 4 * gq:4 * gq + 4, :], hot16[:, 4 * gq:4 * gq + 4, :],
                                   ACT.Copy).then_inc(hot3_w, 1)
                there, g, _, gq = item(i, q, 0)
                if there:
                    hot_turned(g, gq, turnT3, looked3).then_inc(hotT3, 1)
            turns(act, step3, 2)

            for n in range(5):
                act.wait_ge(value_done, n + 1)
                at_least(act, out_done, n - 1)
                e5 = expo[:, (n % 2) * 5 * D:(n % 2 + 1) * 5 * D].rearrange("p (t d) -> p t d", t=5)
                v5 = acc[:, :].rearrange("p (t c) -> p t c", c=AW)[:, 5 * n:5 * n + 5, 0:D]
                act.activation(e5, v5, ACT.Relu, scale=-1.0).then_inc(below, 1)
                act.wait_ge(below, 2 * n + 1)
                act.activation(e5, e5, ACT.Exp, scale=-1.0).then_inc(below, 1)
                act.wait_ge(below, 2 * n + 2)
                act.activation(e5, e5, ACT.Copy, bias=-1.0).then_inc(exp_done, 1)

        @block.vector
        def _(dve):
            linked = [0]

            def link(ins):
                linked[0] += 1
                ins.then_inc(dve_link, 1)
                dve.wait_ge(dve_link, linked[0])

            def norm_tiles(n):
                with dve.Fori(0, TILES) as t:
                    dve.bn_stats(stats[:, bass.ds(t, 1), :].rearrange("p a b -> p (a b)"), xb[:, node_tile(t)])
                link(dve.drain())
                for t in range(TILES):
                    dve.bn_aggr(mv[:, t, :], stats[:, t, :])
                link(dve.drain())
                dve.nop().then_inc(stats_done, 1)
                dve.wait_ge(sqrt_done, n + 1)
                link(dve.reciprocal(rstd[:, :], rstd[:, :]))
                with dve.Fori(0, TILES) as t:
                    dve.tensor_scalar(acc[:, node_tile(t)], xb[:, node_tile(t)],
                                      mv[:, bass.ds(t, 1), 0:1].rearrange("p a b -> p (a b)"),
                                      rstd[:, bass.ds(t, 1)], ALU.subtract, ALU.mult).then_inc(normed, 1)

            real = slice(0, EC)

            def conv_row():
                link(dve.scalar_tensor_tensor(out=tmp_i[:, real], in0=src_i[:, :], scalar=float(R), in1=et_i[:, :],
                                              op0=ALU.mult, op1=ALU.add))
                return tmp_i[:, real]

            def count(n, o, key, payload):
                link(dve.tensor_scalar(tmp_i[:, real], key, SHIFT, None, ALU.arith_shift_right))
                link(dve.tensor_copy(tile_f[:, real], tmp_i[:, real]))
                at_least(dve, counts_summed, n)
                for k in range(TILES):
                    dve.tensor_scalar(o.member[:, k, :], tile_f[:, :], float(k), None, ALU.is_equal, ALU.add,
                                      accum_out=n_in[:, k:k + 1])
                link(dve.drain())
                dve.nop().then_inc(counts_ready, 1)
                link(dve.tensor_scalar(low_i[:, real], key, P - 1, None, ALU.bitwise_and))
                if n == 0:
                    link(dve.tensor_copy(low16[:, real], low_i[:, real]))
                    link(dve.scalar_tensor_tensor(out=tile_rel[:, real], in0=tile_f[:, real], scalar=float(R),
                                                  in1=et_i[:, :], op0=ALU.mult, op1=ALU.add))
                row = payload()
                link(dve.tensor_scalar(tmp2_i[:, real], row, 4, None, ALU.arith_shift_right))
                link(dve.tensor_copy(o.hi[:, real], tmp2_i[:, real]))
                link(dve.tensor_scalar(tmp2_i[:, real], row, 15, None, ALU.bitwise_and))
                link(dve.scalar_tensor_tensor(out=pos[:, real], in0=tmp2_i[:, real], scalar=float(P),
                                              in1=low_i[:, real], op0=ALU.mult, op1=ALU.add))
                link(dve.tensor_scalar(o.lo[:, real], pos[:, real], 1.0, None, ALU.add))

            def place(n, o):
                dve.wait_ge(counts_summed, n + 1)
                link(dve.tensor_scalar(tot_i[:, :], count_ps[:, 0:TILES], float(P - 1), None, ALU.add))
                link(dve.tensor_scalar(tot_i[:, :], tot_i[:, :], SHIFT, None, ALU.arith_shift_right))
                link(dve.tensor_copy(nch[:, :], tot_i[:, :]))
                link(dve.tensor_tensor_scan(cend[:, :], nch[:, :], zeros16[:, 0:TILES], 0.0, ALU.add, ALU.add))
                link(dve.tensor_tensor(start[:, :], cend[:, :], nch[:, :], ALU.subtract))
                link(dve.scalar_tensor_tensor(out=start[:, :], in0=start[:, :], scalar=float(P),
                                              in1=count_ps[:, TILES:2 * TILES], op0=ALU.mult, op1=ALU.add))
                dve.nop().then_inc(counts_read, 1)
                link(dve.tensor_scalar(start[:, :], start[:, :], -1.0, None, ALU.add))
                link(dve.memset(pos[:, :], -1.0))
                link(dve.memset(tid_f[:, :], 0.0))
                for k in range(TILES):
                    link(dve.tensor_tensor_scan(run[:, k % 2, :], o.member[:, k, :], zeros16[0:EP, :],
                                                start[0:EP, k:k + 1], ALU.add, ALU.add))
                    link(dve.copy_predicated(pos[:, :], o.member[:, k, :], run[:, k % 2, :]))
                    link(dve.scalar_tensor_tensor(out=tid_f[:, :], in0=iota16[0:1, 0:CHUNKS], scalar=cend[0:1, k:k + 1],
                                                  in1=tid_f[:, :], op0=ALU.is_ge, op1=ALU.add))
                link(dve.tensor_scalar(o.tid[:, :], tid_f[:, :], float(TILES - 1), None, ALU.min))
                link(dve.tensor_copy(tmp_i[:, :], pos[:, :]))
                link(dve.tensor_scalar(tmp2_i[:, :], tmp_i[:, :], SHIFT, None, ALU.arith_shift_right))
                link(dve.tensor_copy(o.chunk[:, :], tmp2_i[:, :]))
                link(dve.tensor_scalar(tmp2_i[:, :], tmp_i[:, :], P - 1, None, ALU.bitwise_and))
                link(dve.tensor_copy(o.lane[:, :], tmp2_i[:, :]))

            def four(columns, g):
                return columns[:, bass.ds(4 * g, 4)].unsqueeze(1).broadcast_to([EP, P, 4])

            def columns(g, b, o, before_):
                at_least(dve, perm_used, g + before_ - 3)
                dve.tensor_tensor(lanes[:, b, :, :], iota4[0:EP, :, :], four(o.lane, g),
                                  ALU.is_equal).then_inc(perm_lane, 1)
                for u in range(4):
                    dve.tensor_scalar(wide[:, 4 * b + u, :], iota16[0:EP, 0:CHUNKS], o.chunk[:, bass.ds(4 * g + u, 1)],
                                      None, ALU.is_equal)
                dve.wait_ge(perm_lane, g + before_ + 1)
                dve.tensor_tensor(lanes_lo[:, b, :, :], lanes[:, b, :, :], four(o.lo, g),
                                  ALU.mult).then_inc(perm_ready, 1)

            def finish_order(o, n):
                dve.wait_ge(perm_used, GROUPS * (n + 1))
                hi, lo = perm_ps[0][:, 0:CHUNKS], perm_ps[1][:, 0:CHUNKS]
                link(dve.tensor_scalar(slot_i[:, :], lo, -1.0, 0.0, ALU.add, ALU.max))
                link(dve.tensor_scalar(slot2_i[:, :], slot_i[:, :], SHIFT, None, ALU.arith_shift_right))
                link(dve.scalar_tensor_tensor(out=o.idx[:, 0:CHUNKS], in0=hi, scalar=16.0, in1=slot2_i[:, :],
                                              op0=ALU.mult, op1=ALU.add))
                link(dve.tensor_scalar(empty[:, :], lo, 0.0, None, ALU.is_equal))
                link(dve.tensor_scalar(slot2_i[:, :], slot_i[:, :], P - 1, None, ALU.bitwise_and))
                link(dve.scalar_tensor_tensor(out=o.loc[:, :], in0=empty[:, :], scalar=-float(P), in1=slot2_i[:, :],
                                              op0=ALU.mult, op1=ALU.add))
                if n == 0:
                    link(dve.tensor_scalar(slot2_i[:, :], o.idx[:, 0:CHUNKS], R - 1, None, ALU.bitwise_and))
                    link(dve.tensor_copy(et_f[:, :], slot2_i[:, :]))
                dve.nop().then_inc(order_done, 1)

            link(dve.memset(zeros16[:, :], 0.0))
            link(dve.memset(xb[:, (TILES - 1) * D:], 0.0))
            link(dve.memset(eps_col[:, :], EPS_LN))
            link(dve.memset(ones[:, :], 1.0))
            link(dve.memset(tile_f[:, :], -1.0))
            for o in orders:
                link(dve.memset(o.hi[:, :], 0.0))
                link(dve.memset(o.lo[:, :], 0.0))
                link(dve.memset(o.idx[:, CHUNKS:], 0))
            dve.wait_ge(pool_const, 3)
            link(dve.tensor_scalar(ident[:, :], iota16[:, 0:P], lane_no[:, 0:1], None, ALU.is_equal))
            link(dve.tensor_scalar(ident16[:, :], iota16[:, 0:P], lane_no[:, 0:1], None, ALU.is_equal))
            link(dve.tensor_scalar(before[:, :], iota16[:, 0:P], lane_no[:, 0:1], None, ALU.is_gt))
            link(dve.tensor_scalar(head_w[:, 0:OD], iota16[0:OD, 0:OD], lane_no[0:OD, 0:1], None, ALU.is_equal))
            dve.nop().then_inc(const_done, 1)

            dve.wait_ge(e_in, 48)
            count(0, by_dst, dst_i[:, :], conv_row)
            dve.wait_ge(x_in, 32)
            norm_tiles(0)
            count(1, by_src, src_i[:, :], lambda: dst_i[:, :])
            place(0, by_dst)
            place(1, by_src)
            dve.wait_ge(b_in, 48)

            def hist_block(i, b):
                g = 4 * i + b
                at_least(dve, hist_used, g - 3)
                dve.tensor_tensor(lanes[:, b, :, :], iota4[0:EP, :, :], four(low16, g), ALU.is_equal)
                for u in range(4):
                    last = dve.tensor_scalar(wide[:, 4 * b + u, 0:HC], iota16[0:EP, 0:HC],
                                             tile_rel[:, bass.ds(4 * g + u, 1)], None, ALU.is_equal)
                last.then_inc(hist_ready, 1)
                if b == 3:
                    dve.wait_ge(root_out, i + 1)
                    at_tile = acc[:, node_tile(i)]
                    dve.tensor_tensor(at_tile, at_tile, bias1[:, :], ALU.add)
            turns(dve, hist_block, 0, EC // 4, 4)

            dve.wait_ge(hist_used, EC // 4)
            turns(dve, lambda i, q: columns(4 * i + q, q, by_dst, 0), 0)
            link(dve.tensor_scalar(rcnt[:, :], hist_ps[:, 0:HC], 1.0, None, ALU.max))
            link(dve.reciprocal(rcnt[:, :], rcnt[:, :]))
            dve.nop().then_inc(rcnt_done, 1)
            finish_order(by_dst, 0)

            def add_sum(g, u, ids, source, added, target, width):
                at_least(dve, added, 4 * g + u)
                to = target[:, node_tile(ids[u], width)]
                dve.tensor_tensor(to, source, to, ALU.add).then_inc(added, 1)

            def conv_sum(gq, u):
                return bank[2 * (gq % 2) + u // 2][:, (u % 2) * D:(u % 2 + 1) * D]

            def step1(i, q):
                there, g, _, gq = item(i, q, 0)
                if there:
                    at_least(dve, hot_w, g - 3)
                    for u in range(4):
                        last = dve.tensor_scalar(hot16[:, 4 * gq + u, :], iota16[:, 0:P],
                                                 by_dst.loc[:, bass.ds(4 * g + u, 1)], None, ALU.is_equal)
                    last.then_inc(hot_ready, 1)
                there, g, _, gq = item(i, q, 2)
                if there:
                    dve.wait_ge(looked, g + 1)
                    at_least(dve, picked, g)
                    for u in range(4):
                        last = dve.scalar_tensor_tensor(out=trash[:, u, :], in0=iota16[:, 0:R],
                                                        scalar=et_f[:, bass.ds(4 * g + u, 1)],
                                                        in1=bank[4 + gq % 2][:, u * R:(u + 1) * R], op0=ALU.is_equal,
                                                        op1=ALU.mult, accum_out=weight[:, bass.ds(4 * g + u, 1)])
                    last.then_inc(picked, 1)
                there, g, _, gq = item(i, q, 4)
                if there:
                    ids = tile_ids(DVE, by_dst, g)
                    dve.wait_ge(summed1, g + 1)
                    for u in range(4):
                        add_sum(g, u, ids, conv_sum(gq, u), added1, acc, D)
            turns(dve, step1, 4)

            with dve.Fori(0, TILES) as t:
                dve.tensor_tensor(xb[:, node_tile(t)], xb[:, node_tile(t)], bias2[:, :], ALU.add)
            link(dve.drain())

            def root2(i, q):
                t = 5 * i + q
                dve.wait_ge(root_prod, t + 1 + TILES)
                dve.tensor_tensor(xb[:, node_tile(t)], root_ps[:, 0:D], xb[:, node_tile(t)],
                                  ALU.add).then_inc(root_out, 1)
            turns(dve, root2, 0, TILES, 5)
            dve.wait_ge(root_out, 2 * TILES)

            def step2(i, q):
                here, g, _, gq = item(i, q, 0)
                there2, g2, _, gq2 = item(i, q, 2)
                if there2:
                    ids = tile_ids(DVE, by_dst, g2)
                if here:
                    at_least(dve, summed2, g - 3)
                if there2:
                    dve.wait_ge(summed2, g2 + 1)
                for u in range(4):
                    if here:
                        last = dve.tensor_scalar(hot[:, 4 * gq + u, :], iota16[:, 0:P],
                                                 by_dst.loc[:, bass.ds(4 * g + u, 1)],
                                                 weight[:, bass.ds(4 * g + u, 1)], ALU.is_equal, ALU.mult)
                        if u == 3:
                            last.then_inc(hot2, 1)
                    if there2:
                        add_sum(g2, u, ids, conv_sum(gq2, u), added2, xb, D)
                if here:
                    columns(g, gq, by_src, GROUPS)
            turns(dve, step2, 2)
            dve.wait_ge(added2, CHUNKS)

            norm_tiles(1)
            finish_order(by_src, 1)

            def table_rows(i, q):
                t = 5 * i + q
                dve.wait_ge(tab_prod, t + 1)
                dve.tensor_copy(tabst[:, bass.ds(t, 1), :].rearrange("p a c -> p (a c)"), bank[1][:, 0:TW])
                dve.tensor_copy(el_tab[:, node_tile(t, HEADS)], bank[1][:, TW:TW + HEADS]).then_inc(tab_out, 1)
            turns(dve, table_rows, 0, TILES, 5)
            dve.wait_ge(fed, 3 * TILES)
            link(dve.memset(acc[:, :], 0.0))

            def scores(g, gi, gq):
                for u in range(4):
                    dve.wait_ge(landed[4 * gq + u], 16 * (gi + 1 + 2 * TURNS))
                dve.wait_ge(looked3, g + 1)
                at_least(dve, e_done, g - 3)
                dve.tensor_tensor(zbuf[:, gq, :, :],
                                  bank[4 + gq % 2][:, 0:4 * HEADS].rearrange("p (u h) -> p u h", u=4),
                                  arows[:, 4 * gq:4 * gq + 4, OD:TW], ALU.add).then_inc(z_sum, 1)
                dve.wait_ge(z_sum, g + 1)
                zf = zbuf[:, gq, :, :].rearrange("p u h -> p (u h)")
                dve.scalar_tensor_tensor(out=zf, in0=zf, scalar=SLOPE, in1=zf, op0=ALU.mult,
                                         op1=ALU.max).then_inc(z_done, 1)

            def step3(i, q):
                here, g, _, gq = item(i, q, 0)
                there2, g2, gi2, gq2 = item(i, q, 2)
                there3, g3, _, gq3 = item(i, q, 3)
                there5, g5, _, gq5 = item(i, q, 5)
                if there5:
                    ids = tile_ids(DVE, by_src, g5)
                if here:
                    at_least(dve, hot3_w, g - 3)
                for u in range(4):
                    if here:
                        ins = dve.tensor_scalar(hot16[:, 4 * gq + u, :], iota16[:, 0:P],
                                                by_src.loc[:, bass.ds(4 * g + u, 1)], None, ALU.is_equal)
                        if u == 3:
                            ins.then_inc(hot3, 1)
                    if there5:
                        dve.wait_ge(summed3, 4 * g5 + u + 1)
                        add_sum(g5, u, ids, bank[u][:, 0:AW], added3, acc, AW)
                    if there3:
                        s = 4 * gq3 + u
                        dve.wait_ge(e_done, g3 + 1)
                        ins = dve.tensor_tensor(
                            arhs[:, s, 0:D].rearrange("p (h o) -> p h o", h=HEADS),
                            arows[:, s, 0:OD].unsqueeze(1).broadcast_to([P, HEADS, OD]),
                            arhs[:, s, D:AW].unsqueeze(2).broadcast_to([P, HEADS, OD]), ALU.mult)
                        if u == 3:
                            ins.then_inc(rhs_done, 1)
                    if there2 and u == 1:
                        scores(g2, gi2, gq2)
            turns(dve, step3, 5)

            dve.wait_ge(added3, CHUNKS)
            av = acc[:, :].rearrange("p (t c) -> p t c", c=AW)
            rsum = tabst[:, :, 0:HEADS]
            dve.wait_ge(tab_stored, 80)
            link(dve.tensor_scalar(rsum, av[:, :, D:AW], EPS_ROW, None, ALU.max))
            link(dve.reciprocal(rsum, rsum))
            for n in range(6):
                if n < 5:
                    ts = slice(5 * n, 5 * n + 5)
                    v = av[:, ts, 0:D].rearrange("p t (h o) -> p t h o", h=HEADS)
                    link(dve.tensor_tensor(v, v, rsum[:, ts, :].unsqueeze(3).broadcast_to([P, 5, HEADS, OD]), ALU.mult))
                    dve.tensor_tensor(v, v, biasg[:, :].unsqueeze(1).unsqueeze(1).broadcast_to([P, 5, HEADS, OD]),
                                      ALU.add).then_inc(value_done, 1)
                if n:
                    dve.wait_ge(exp_done, n)
                    e5 = expo[:, ((n - 1) % 2) * 5 * D:((n - 1) % 2 + 1) * 5 * D].rearrange("p (t d) -> p t d", t=5)
                    v5 = av[:, 5 * n - 5:5 * n, 0:D]
                    dve.scalar_tensor_tensor(out=e5, in0=v5, scalar=0.0, in1=e5, op0=ALU.max,
                                             op1=ALU.add).then_inc(plus_done, 1)


_INS = ["x", "src", "dst", "edge_type_8", "L0_gnn_W1", "L0_gnn_Wroot1", "L0_gnn_b1", "L0_gnn_W2", "L0_gnn_Wroot2",
        "L0_gnn_b2", "L1_gnn_W", "L1_gnn_Wl", "L1_gnn_Wr", "L1_gnn_b"]


def kernel(**inputs):
    import concourse.bacc as bacc
    from concourse.bass_utils import run_bass_kernel_spmd

    nc = bacc.Bacc("TRN2", target_bir_lowering=False, num_devices=1)
    arrays, args = {}, []
    for name in _INS:
        a = np.ascontiguousarray(inputs[name])
        arrays[f"in_{name}"] = a
        args.append(nc.dram_tensor(f"in_{name}", a.shape, mybir.dt.from_np(a.dtype), kind="ExternalInput").ap())
    shape = inputs["x"].shape
    args.append(nc.dram_tensor("out_0", shape, F32, kind="ExternalOutput").ap())
    build_gnn(nc, *args)
    r = run_bass_kernel_spmd(nc, [arrays], core_ids=[0])
    return r.results[0]["out_0"]
```

```python
from contextlib import ExitStack

import numpy as np

import concourse.bass as bass
from concourse import mybir

F32 = mybir.dt.float32
F16 = mybir.dt.float16
I32 = mybir.dt.int32
U8 = mybir.dt.uint8
ALU = mybir.AluOpType
ACT = mybir.ActivationFunctionType
PE = mybir.EngineType.PE
DVE = mybir.EngineType.DVE

P = 128
SHIFT = 7


def build_gnn(nc, x, src, dst, etype, W1, Wroot1, b1, W2, Wroot2, b2, Wg, Wl, Wr, bg, out):
    N, D = x.shape
    E = src.shape[0]
    R = W1.shape[0]
    OD, HEADS = Wg.shape[1], Wl.shape[0]
    TILES = -(-N // P)
    TAIL = N - (TILES - 1) * P
    KH = D // P
    EP = next(p for p in range(P, 0, -1) if E % p == 0)
    EC = E // EP
    CHUNKS = -(-(E // P + TILES) // 16) * 16
    GROUPS = CHUNKS // 4
    TURNS = GROUPS // 4
    PLAIN_TURNS = 2
    assert TILES % 5 == 0 and GROUPS % 8 == 0 and EC % 16 == 0
    assert CHUNKS >= EC and CHUNKS >= E // P + TILES and CHUNKS <= 512
    assert KH == 2 and HEADS * OD == D
    YC = R * D // 512
    HIST_BLOCKS, PERM_BLOCKS = (2, 3) * (YC // 2), (2,) * YC
    BESIDE = {PLAIN_TURNS: ("hist", HIST_BLOCKS, 0), PLAIN_TURNS + 1: ("hist", HIST_BLOCKS, 5 * sum(HIST_BLOCKS)),
              PLAIN_TURNS + 2: ("perm", PERM_BLOCKS, 0)}
    PERM_BESIDE = 5 * sum(PERM_BLOCKS)
    SCATTERED = EC // 4 - PERM_BESIDE - 8
    DST_BLOCKS = EC // 4 - SCATTERED
    assert PLAIN_TURNS + 3 == TILES // 5 and 10 * sum(HIST_BLOCKS) == EC // 4 and PERM_BESIDE % 4 == 0
    assert SCATTERED > 0 and SCATTERED % 4 == 0 and DST_BLOCKS % 4 == 0
    HC = TILES * R
    TW = OD + HEADS
    AW = D + HEADS
    EPS_LN, EPS_ROW, SLOPE = 1e-5, 1e-12, 0.2

    y_dram = nc.dram_tensor("y_rows", (TILES * P * R, D), F32, kind="Internal").ap()
    tab_dram = nc.dram_tensor("attention_rows", (TILES * P, TW), F32, kind="Internal").ap()
    slots_dram = nc.dram_tensor("slots", (P * CHUNKS, 1), I32, kind="Internal").ap()
    slots_rows = slots_dram.rearrange("(p c) o -> p (c o)", p=P)
    y_tiles = y_dram.rearrange("(t p r) d -> p t (r d)", p=P, r=R)
    tab_tiles = tab_dram.rearrange("(t p) c -> p t c", p=P)

    with ExitStack() as ctx:
        def sb(name, shape, dt):
            return ctx.enter_context(nc.sbuf_tensor(name, shape, dt))

        def sem(name):
            return ctx.enter_context(nc.semaphore(name))

        bank = [ctx.enter_context(nc.psum_tensor(f"bank{i}", [P, 512], F32)) for i in range(6)]
        turn16 = [ctx.enter_context(nc.psum_tensor(f"turn16_{i}", [P, 1024], F16)) for i in range(2)]
        root_ps, turn_ps, count_ps, hist_ps = bank[2:6]
        x1_ps, tab_ps = (bank[0], bank[1]), (bank[2], bank[4])
        turn3_ps = (turn_ps, bank[5])
        perm_ps = [t[:, :].bitcast(F32) for t in turn16]

        iota16 = sb("iota16", [P, 512], F16)
        iota4 = sb("iota4", [P, P, 4], F16)
        lane_no = sb("lane_no", [P, 1], F32)
        ident = sb("ident", [P, P], F32)
        ident16 = sb("ident16", [P, P], F16)
        before = sb("before", [P, P], F32)
        ones = sb("ones", [P, P], F32)
        zeros16 = sb("zeros16", [P, CHUNKS], F16)
        eps_col = sb("eps_col", [P, 1], F32)
        bias1 = sb("bias1", [P, D], F32)
        bias2 = sb("bias2", [P, D], F32)
        biasg = sb("biasg", [P, OD], F32)

        xb = sb("xb", [P, TILES * D], F32)
        acc = sb("acc", [P, TILES * AW], F32)
        feed = sb("feed", [P, 5, D], F32)
        hT = sb("hT", [P, 5, D], F32)
        w_sb = sb("w_sb", [P, KH, R * D], F32)
        wroot_sb = sb("wroot_sb", [P, KH, D], F32)
        stats = sb("stats", [P, TILES, 6], F32)
        mv = sb("mv", [P, TILES, 2], F32)
        warm = sb("warm", [P, 1], F32)
        rstd = sb("rstd", [P, TILES], F32)
        rcnt = sb("rcnt", [P, HC], F32)
        wg_sb = sb("wg_sb", [P, KH, OD], F32)
        head_w = sb("head_w", [OD, OD + 2 * HEADS], F32)
        x1T = sb("x1T", [OD, 5, P], F32)
        tabst = sb("tabst", [P, TILES, TW], F32)
        el_tab = sb("el_tab", [P, TILES * HEADS], F32)

        src_i = sb("src_i", [EP, EC], I32)
        dst_i = sb("dst_i", [EP, EC], I32)
        et_i = sb("et_i", [EP, EC], I32)
        lists = sb("lists", [EP, 9, CHUNKS], F32)
        tmp_i, tmp2_i, low_i = (lists[:, k, :].bitcast(I32) for k in range(3))
        tile_f, pos, tile_rel = (lists[:, k, :] for k in range(3, 6))
        run = lists[:, 6:8, :]
        low16 = lists[:, 8, 0:CHUNKS // 2].bitcast(F16)
        scatter_list = sb("scatter_list", [EP, 4 * (SCATTERED + 1), 2], I32)
        scatter_ring = sb("scatter_ring", [EP, 16, 2], I32)
        n_in = sb("n_in", [EP, TILES], F32)
        tot_i = sb("tot_i", [P, TILES], I32)
        nch = sb("nch", [P, TILES], F32)
        cend = sb("cend", [P, TILES], F32)
        start = sb("start", [P, TILES], F32)
        tid_f = sb("tid_f", [1, CHUNKS], F32)

        class Order:
            pass
        orders = []
        for name in ("dst", "src"):
            o = Order()
            o.chunk = sb(f"{name}_chunk", [EP, CHUNKS], F32)
            o.lane = sb(f"{name}_lane", [EP, CHUNKS], F16)
            o.hi = sb(f"{name}_hi", [EP, CHUNKS], F32)
            o.lo = sb(f"{name}_lo", [EP, CHUNKS], F16 if name == "dst" else F32)
            o.tid = sb(f"{name}_tid", [1, CHUNKS], I32)
            o.idx = sb(f"{name}_idx", [P, CHUNKS + 16], I32)
            o.loc = sb(f"{name}_loc", [P, CHUNKS], F32)
            orders.append(o)
        by_dst, by_src = orders
        et_f = sb("et_f", [P, CHUNKS], F32)
        weight = sb("weight", [P, CHUNKS], F32)
        slot_i = sb("slot_i", [P, CHUNKS], I32)
        slot2_i = sb("slot2_i", [P, CHUNKS], I32)
        empty = sb("empty", [P, CHUNKS], F32)

        cols = sb("cols", [P, 8 * CHUNKS + 3 * 8 * P], F32)
        wide = cols[0:EP, 0:8 * CHUNKS].bitcast(F16).rearrange("p (s c) -> p s c", c=CHUNKS)
        lanes, lanes_hi, lanes_lo = (cols[0:EP, 8 * (CHUNKS + k * P):8 * (CHUNKS + (k + 1) * P)].bitcast(F16)
                                     .rearrange("p (b l u) -> p b l u", b=4, u=4) for k in range(3))
        for n, o in enumerate(orders):
            o.member = cols[0:EP, n * TILES * CHUNKS // 4:(n + 1) * TILES * CHUNKS // 4].bitcast(U8).rearrange(
                "p (k c) -> p k c", c=CHUNKS)
        arhs = cols[:, 0:16 * AW].rearrange("p (s c) -> p s c", c=AW)
        arows = cols[:, 16 * AW:16 * (AW + TW)].rearrange("p (s c) -> p s c", c=TW)
        rows = sb("rows", [P, 16, D], F32)
        ystage = rows[:, :, :].rearrange("p s d -> p (s d)").rearrange("p (n w) -> p n w", w=512)
        idx_ring = sb("idx_ring", [P, 32], I32)
        hot = sb("hot", [P, 16, P], F32)
        hots = sb("hots", [P, 16 * P], F32)
        hot16 = hots[:, 0:8 * P].bitcast(F16).rearrange("p (s n) -> p s n", n=P)
        hotT = hots[:, 8 * P:16 * P].rearrange("p (a n) -> p a n", a=2)
        zbuf = sb("zbuf", [P, 4, 4, HEADS], F32)
        trash = sb("trash", [P, 4, R], F32)
        expo = rows[:, :, :].rearrange("p s d -> p (s d)")

        x_first, x_in, e_in, b_in = sem("x_first"), sem("x_in"), sem("e_in"), sem("b_in")
        w1_in, w2_in, wg_in = sem("w1_in"), sem("w2_in"), sem("wg_in")
        pool_const, const_done = sem("pool_const"), sem("const_done")
        dve_link = sem("dve_link")
        stats_done, sqrt_done = sem("stats_done"), sem("sqrt_done")
        normed = sem("normed")
        fed, turned, hT_done = sem("fed"), sem("turned"), sem("hT_done")
        y_prod = sem("y_prod")
        y_out = sem("y_out")
        y_stored = [sem(f"y_stored{n}") for n in range(YC)]
        root_prod, root_out = sem("root_prod"), sem("root_out")
        counts_ready = sem("counts_ready")
        counts_summed, counts_read = sem("counts_summed"), sem("counts_read")
        hist_ready, hist_used = sem("hist_ready"), sem("hist_used")
        rcnt_done = sem("rcnt_done")
        perm_lane, perm_ready = sem("perm_lane"), sem("perm_ready")
        perm_hi, perm_used = sem("perm_hi"), sem("perm_used")
        idx_done, order_done = sem("idx_done"), sem("order_done")
        acc_zeroed, x_less_one = sem("acc_zeroed"), sem("x_less_one")
        slots_zeroed, slots_in = sem("slots_zeroed"), sem("slots_in")
        scatter_ready, scatter_placed = sem("scatter_ready"), sem("scatter_placed")
        scattered = [sem(f"scattered{q}") for q in range(4)]
        idx_placed, pool_passed = sem("idx_placed"), sem("pool_passed")
        act_passed = sem("act_passed")
        landed = [sem(f"landed{s}") for s in range(16)]
        hot_ready, turnT, hotT_done = sem("hot_ready"), sem("turnT"), sem("hotT_done")
        looked, picked, hot_w = sem("looked"), sem("picked"), sem("hot_w")
        summed1, added1 = sem("summed1"), sem("added1")
        hot2, summed2, added2 = sem("hot2"), sem("summed2"), sem("added2")
        x1_prod, x1_out, tab_prod, tab_out = sem("x1_prod"), sem("x1_out"), sem("tab_prod"), sem("tab_out")
        tab_stored = sem("tab_stored")
        hot3, turnT3, hotT3, looked3 = sem("hot3"), sem("turnT3"), sem("hotT3"), sem("looked3")
        z_sum, z_done, e_done, rhs_done = sem("z_sum"), sem("z_done"), sem("e_done"), sem("rhs_done")
        hot3_w, summed3, added3 = sem("hot3_w"), sem("summed3"), sem("added3")
        value_done, below, plus_done = sem("value_done"), sem("below"), sem("plus_done")
        exp_done, out_done, out_stored = sem("exp_done"), sem("out_done"), sem("out_stored")

        def at_least(eng, s, value):
            if not (isinstance(value, int) and value <= 0):
                eng.wait_ge(s, value)

        def turns(eng, step, lag, count=GROUPS, ring=4, peel=0):
            first = peel or (2 if lag >= 2 else 1)
            for i in range(first):
                for q in range(ring):
                    step(i, q)
            with eng.Fori(first, count // ring) as i:
                for q in range(ring):
                    step(i, q)
            for q in range(lag):
                step(count // ring, q)

        def item(i, q, lag, count=GROUPS, ring=4):
            i2, q2 = i + (q - lag) // ring, (q - lag) % ring
            there = not isinstance(i, int) or 0 <= ring * i2 + q2 < count
            return there, ring * i2 + q2, i2, q2

        def tile_ids(engine, o, g):
            _, ids = nc.values_load_multi_w_load_instructions(
                o.tid[0:1, bass.ds(4 * g, 4)], engines=[engine], min_val=0, max_val=TILES - 1,
                skip_runtime_bounds_check_because="the ids are clamped to TILES - 1 when they are made")
            return ids

        def node_tile(t, width=D):
            return bass.ds(t * width, width)

        def block_numbers(q, n, blocks, first):
            at = first + q * sum(blocks) + sum(blocks[:n])
            return range(at, at + blocks[n])

        def root_tile(i, lag=0):
            there = not isinstance(i, int) or lag < i <= TILES + lag
            return there, i - 1 - lag

        block = ctx.enter_context(nc.Block())

        @block.sync
        def _(sp):
            def load_x(first, last, done):
                sp.dma_start(xb[:, first * D:last * D].rearrange("p (t d) -> p t d", d=D),
                             x[first * P:last * P, :].rearrange("(t p) d -> p t d", p=P)).then_inc(done, 16)

            load_x(0, 5, x_first)
            sp.dma_start(dst_i[:, :], dst.rearrange("(p c) -> p c", p=EP)).then_inc(e_in, 16)
            sp.dma_start(src_i[:, :], src.rearrange("(p c) -> p c", p=EP)).then_inc(e_in, 16)
            sp.dma_start(et_i[:, :], etype.rearrange("(p c) -> p c", p=EP)).then_inc(e_in, 16)
            def load_weights(W, Wroot, done):
                for k in range(KH):
                    sp.dma_start(w_sb[:, k, :].rearrange("p (r e) -> p r e", r=R),
                                 W[:, k * P:(k + 1) * P, :].rearrange("r p e -> p r e")).then_inc(done, 16)
                sp.dma_start(wroot_sb[:, :, :], Wroot.rearrange("(k p) e -> p k e", p=P)).then_inc(done, 16)

            load_weights(W1, Wroot1, w1_in)
            sp.wait_ge(const_done, 1)
            sp.dma_start(slots_rows, slot_i[:, :]).then_inc(slots_zeroed, 16)
            load_x(5, TILES - 1, x_in)
            sp.dma_start(xb[0:TAIL, (TILES - 1) * D:], x[(TILES - 1) * P:, :]).then_inc(x_in, 16)
            sp.dma_start(bias1[:, :], b1.unsqueeze(0).broadcast_to([P, D])).then_inc(b_in, 16)
            sp.dma_start(bias2[:, :], b2.unsqueeze(0).broadcast_to([P, D])).then_inc(b_in, 16)
            sp.dma_start(biasg[:, :], bg.unsqueeze(0).broadcast_to([P, OD])).then_inc(b_in, 16)
            sp.dma_start(wg_sb[:, :, :], Wg.rearrange("(k p) e -> p k e", p=P)).then_inc(wg_in, 16)
            with nc.allow_non_contiguous_dma(reason="two 64 x 4 matrices, turned"):
                sp.dma_start(head_w[:, OD:OD + HEADS], Wr.rearrange("h o -> o h")).then_inc(wg_in, 16)
                sp.dma_start(head_w[:, OD + HEADS:], Wl.rearrange("h o -> o h")).then_inc(wg_in, 16)

            def store_y(layer):
                with sp.Fori(0, TILES) as t:
                    for n in range(YC):
                        sp.wait_ge(y_out, (t + layer * TILES) * YC + n + 1)
                        sp.dma_start(y_tiles[:, bass.ds(t, 1), n * 512:(n + 1) * 512],
                                     ystage[:, n:n + 1, :]).then_inc(y_stored[n], 16)

            store_y(0)
            sp.wait_ge(root_prod, TILES)
            load_weights(W2, Wroot2, w2_in)
            sp.wait_ge(added1, CHUNKS)
            store_y(1)

            for n in range(5):
                sp.wait_ge(tab_out, (n + 1) * TILES // 5)
                part = slice(n * TILES // 5, (n + 1) * TILES // 5)
                sp.dma_start(tab_tiles[:, part, :], tabst[:, part, :]).then_inc(tab_stored, 16)

            for t in range(0, TILES, 5):
                sp.wait_ge(out_done, t // 5 + 1)
                last = t + 5 >= TILES
                full = TILES - 1 - t if last else 5
                sp.dma_start(out[t * P:(t + full) * P, :].rearrange("(t p) d -> p t d", p=P),
                             xb[:, t * D:(t + full) * D].rearrange("p (t d) -> p t d", d=D)).then_inc(out_stored, 16)
                if last:
                    sp.dma_start(out[(TILES - 1) * P:, :], xb[0:TAIL, (TILES - 1) * D:]).then_inc(out_stored, 16)
            sp.wait_ge(out_stored, 16 * (-(-TILES // 5) + 1))

        @block.gpsimd
        def _(pool):
            pool.iota(iota16[:, :], [[1, 512]], base=0, channel_multiplier=0,
                      allow_small_or_imprecise_dtypes=True).then_inc(pool_const, 1)
            pool.iota(iota4[:, :, :], [[1, P], [0, 4]], base=0, channel_multiplier=0,
                      allow_small_or_imprecise_dtypes=True).then_inc(pool_const, 1)
            pool.iota(lane_no[:, :], [[1, 1]], base=0, channel_multiplier=1,
                      allow_small_or_imprecise_dtypes=True).then_inc(pool_const, 1)

            def scatter():
                def place(q, g, turn):
                    at_least(pool, scattered[q], 64 * turn)
                    pool.tensor_copy(scatter_ring[:, 4 * q:4 * q + 4, :],
                                     scatter_list[:, bass.ds(4 * g, 4), :]).then_inc(scatter_placed, 1)

                def step(i, q):
                    g = 4 * i + q
                    pool.wait_ge(scatter_placed, g + 1)
                    pool.sem_inc(pool_passed, 1)
                    for u in range(4):
                        if u == 2:
                            place((q + 1) % 4, g + 1, i if q < 3 else i + 1)
                        s = 4 * q + u
                        pool.indirect_dma_start(
                            out=slots_dram, out_offset=bass.IndirectOffsetOnAxis(ap=scatter_ring[:, s, 0:1], axis=0),
                            in_=scatter_ring[:, s, 1:2], in_offset=None).then_inc(scattered[q], 16)
                pool.wait_ge(slots_zeroed, 16)
                pool.wait_ge(scatter_ready, 1)
                place(0, 0, 0)
                turns(pool, step, 0, SCATTERED)
                for q in range(4):
                    pool.wait_ge(scattered[q], 16 * SCATTERED)
                pool.dma_start(slot_i[:, :], slots_rows).then_inc(slots_in, 16)

            def gather(layer, o, table, ring, used):
                def place(half, g):
                    pool.tensor_copy(idx_ring[:, 16 * half:16 * half + 16],
                                     o.idx[:, bass.ds(4 * g, 16)]).then_inc(idx_placed, 1)

                placed_before = layer * (GROUPS // 4 + 1)

                def step(i, q):
                    g = 8 * i + q
                    at_least(pool, used, g - 3)
                    if q % 4 == 0:
                        pool.sem_inc(pool_passed, 1)
                        pool.wait_ge(idx_placed, 2 * i + q // 4 + 1 + placed_before)
                    pool.sem_inc(pool_passed, 1)
                    for u in range(4):
                        if u == 2 and q % 4 == 3:
                            place((q + 1) // 4 % 2, g + 1)
                        s = 4 * (q % 4) + u
                        pool.indirect_dma_start(
                            out=ring[:, s, :], out_offset=None, in_=table,
                            in_offset=bass.IndirectOffsetOnAxis(ap=idx_ring[:, 4 * q + u:4 * q + u + 1], axis=0),
                        ).then_inc(landed[s], 16)
                at_least(pool, idx_placed, placed_before)
                place(0, 0)
                turns(pool, step, 0, GROUPS, 8)

            scatter()
            pool.wait_ge(idx_done, 1)
            for n in range(YC):
                pool.wait_ge(y_stored[n], 16 * TILES)
            gather(0, by_dst, y_dram, rows, summed1)
            for n in range(YC):
                pool.wait_ge(y_stored[n], 32 * TILES)
            gather(1, by_dst, y_dram, rows, summed2)
            pool.wait_ge(fed, 3 * TILES)
            pool.memset(acc[:, :], 0.0).then_inc(acc_zeroed, 1)
            for n in range(5):
                pool.wait_ge(fed, 3 * TILES + 5 * (n + 1))
                xs = xb[:, 5 * n * D:5 * (n + 1) * D]
                pool.tensor_scalar(xs, xs, -1.0, None, ALU.add).then_inc(x_less_one, 1)
            pool.wait_ge(idx_done, 2)
            pool.wait_ge(tab_stored, 80)
            gather(2, by_src, tab_dram, arows, rhs_done)

            for n in range(4):
                pool.wait_ge(plus_done, n + 1)
                pool.wait_ge(x_less_one, n + 1)
                xs = xb[:, 5 * n * D:5 * (n + 1) * D]
                pool.tensor_tensor(xs, xs, expo[:, (n % 2) * 5 * D:(n % 2 + 1) * 5 * D], ALU.add).then_inc(out_done, 1)

        @block.tensor
        def _(pe):
            def turn(t, place, ps, phase, since=1):
                pe.wait_ge(fed, t + 1 + phase * TILES)
                at_least(pe, hT_done, t + 1 - since + phase * TILES)
                for k in range(KH):
                    last = pe.transpose(ps[:, k * P:(k + 1) * P], feed[:, place, k * P:(k + 1) * P], ident[:, :])
                last.then_inc(turned, 1)

            def turn_tile(i, q, phase):
                there, t, _, tq = item(i, q, 0, TILES, 5)
                if there:
                    turn(t, tq, turn_ps, phase)

            def root_product(ps, place):
                for k in range(KH):
                    last = pe.matmul(ps[:, 0:D], hT[:, place, k * P:(k + 1) * P], wroot_sb[:, k, :],
                                     start=(k == 0), stop=(k == KH - 1))
                last.then_inc(root_prod, 1)

            def product_tile(i, q, layer, beside=None):
                there, t, _, tq = item(i, q, 1, TILES, 5)
                if there:
                    pe.wait_ge(hT_done, t + 1 + layer * TILES)
                    for n in range(YC):
                        at_least(pe, y_out, (t + layer * TILES) * YC + n - 1)
                        for k in range(KH):
                            last = pe.matmul(bank[n % 2][:, :], hT[:, tq, k * P:(k + 1) * P],
                                             w_sb[:, k, n * 512:(n + 1) * 512], start=(k == 0), stop=(k == KH - 1))
                        last.then_inc(y_prod, 1)
                        if beside:
                            beside(n)
                    if layer == 0:
                        at_least(pe, root_out, t)
                        root_product(root_ps, tq)

            def histogram(c4, b):
                pe.wait_ge(hist_ready, c4 + 1)
                for u in range(4):
                    last = pe.matmul(hist_ps[:, 0:HC], lanes[:, b, :, u], wide[:, 4 * b + u, 0:HC],
                                     start=False, stop=False, skip_group_check=True)
                last.then_inc(hist_used, 1)

            def permute(c4, b):
                pe.wait_ge(perm_ready, c4 + 1)
                pe.wait_ge(perm_hi, c4 + 1)
                for u in range(4):
                    pe.matmul(perm_ps[0][:, 0:CHUNKS], lanes_hi[:, b, :, u], wide[:, 4 * b + u, :],
                              start=False, stop=False, skip_group_check=True)
                    last = pe.matmul(perm_ps[1][:, 0:CHUNKS], lanes_lo[:, b, :, u], wide[:, 4 * b + u, :],
                                     start=False, stop=False, skip_group_check=True)
                last.then_inc(perm_used, 1)

            def open_sum(ps, width):
                pe.matmul(ps[:, 0:width], zeros16[:, 0:P], zeros16[:, 0:width], start=True, stop=False,
                          skip_group_check=True)

            def sum_counts(n):
                pe.wait_ge(counts_ready, n + 1)
                at_least(pe, counts_read, n)
                pe.matmul(count_ps[:, 0:TILES], ones[0:EP, :], n_in[:, :], start=True, stop=True)
                pe.matmul(count_ps[:, TILES:2 * TILES], before[0:EP, :], n_in[:, :],
                          start=True, stop=True).then_inc(counts_summed, 1)

            pe.wait_ge(const_done, 1)
            pe.wait_ge(w1_in, 16 * (KH + 1))

            def layer1(i, q):
                turn_tile(i, q, 0)
                product_tile(i, q, 0)

            for q in range(5):
                layer1(0, q)
                if q == 2:
                    sum_counts(0)
            with pe.Fori(1, PLAIN_TURNS) as i:
                for q in range(5):
                    layer1(i, q)
            for i, (kind, blocks, first) in BESIDE.items():
                if first == 0:
                    if kind == "hist":
                        open_sum(hist_ps, HC)
                    else:
                        open_sum(perm_ps[0], CHUNKS)
                        open_sum(perm_ps[1], CHUNKS)

                def beside(q, n):
                    for c4 in block_numbers(q, n, blocks, first):
                        (histogram if kind == "hist" else permute)(c4, c4 % 4)
                for q in range(5):
                    turn_tile(i, q, 0)
                    product_tile(i, q, 0, lambda n: beside(q, n))
            layer1(TILES // 5, 0)
            with pe.Fori(PERM_BESIDE // 4, DST_BLOCKS // 4) as i:
                for b in range(4):
                    permute(4 * i + b, b)

            pe.wait_ge(rcnt_done, 1)
            pe.wait_ge(order_done, 1)

            def turn_hot(g, gq, ready, read_out, done):
                pe.wait_ge(ready, g + 1)
                at_least(pe, read_out, g - 1)
                for u in range(4):
                    last = pe.transpose(turn16[gq % 2][:, u * P:(u + 1) * P], hot16[:, 4 * gq + u, :], ident16[:, :])
                last.then_inc(done, 1)

            def look_up(g, gq, ids, table, width, ready, used, done):
                pe.wait_ge(ready, g + 1)
                at_least(pe, used, g - 1)
                for u in range(4):
                    last = pe.matmul(bank[4 + gq % 2][:, u * width:(u + 1) * width],
                                     hotT[:, gq % 2, u * P:(u + 1) * P], table[:, node_tile(ids[u], width)],
                                     start=True, stop=True)
                last.then_inc(done, 1)

            def sum_rows(g, gi, gq, layer, ready, added, done):
                pe.wait_ge(ready, g + 1)
                at_least(pe, added, 4 * (g - 1))
                for u in range(4):
                    s = 4 * gq + u
                    pe.wait_ge(landed[s], 16 * (gi + 1 + layer * TURNS))
                    last = pe.matmul(bank[2 * (gq % 2) + u // 2][:, (u % 2) * D:(u % 2 + 1) * D],
                                     hot[:, s, :], rows[:, s, :], start=True, stop=True)
                last.then_inc(done, 1)

            def step1(i, q):
                there, g, _, gq = item(i, q, 0)
                if there:
                    turn_hot(g, gq, hot_ready, hotT_done, turnT)
                there, g, _, gq = item(i, q, 1)
                if there:
                    look_up(g, gq, tile_ids(PE, by_dst, g), rcnt, R, hotT_done, picked, looked)
                there, g, gi, gq = item(i, q, 3)
                if there:
                    sum_rows(g, gi, gq, 0, hot_w, added1, summed1)
            turns(pe, step1, 3)

            pe.wait_ge(w2_in, 16 * (KH + 1))

            def layer2(i, q):
                turn_tile(i, q, 1)
                product_tile(i, q, 1)
            for q in range(5):
                layer2(0, q)
            sum_counts(1)
            with pe.Fori(1, TILES // 5) as i:
                for q in range(5):
                    layer2(i, q)
            layer2(TILES // 5, 0)

            open_sum(perm_ps[0], CHUNKS)
            open_sum(perm_ps[1], CHUNKS)

            def step2(i, q):
                there, g, gi, gq = item(i, q, 1)
                if there:
                    sum_rows(g, gi, gq, 1, hot2, added2, summed2)
                    permute(g + DST_BLOCKS, gq)
                there, t = root_tile(i)
                if there and q == 1:
                    turn(t, 0, bank[5], 2)
                if there and q == 3:
                    pe.wait_ge(hT_done, t + 1 + 2 * TILES)
                    at_least(pe, root_out, t + TILES)
                    root_product(bank[4], 0)
            pe.wait_ge(counts_read, 2)
            turns(pe, step2, 1, peel=2)

            pe.wait_ge(wg_in, 48)

            def table_rows(i, q):
                there, t, _, tq = item(i, q, 0, TILES, 5)
                if there:
                    turn(t, tq, turn3_ps[tq % 2], 3, 1 if tq == 0 else 2)
                there, t, _, tq = item(i, q, 1, TILES, 5)
                if there:
                    pe.wait_ge(hT_done, t + 1 + 3 * TILES)
                    at_least(pe, x1_out, t if tq == 0 else t - 1)
                    for k in range(KH):
                        last = pe.matmul(x1_ps[tq % 2][0:OD, 0:P], wg_sb[:, k, :], hT[:, tq, k * P:(k + 1) * P],
                                         start=(k == 0), stop=(k == KH - 1))
                    last.then_inc(x1_prod, 1)
                there, t, _, tq = item(i, q, 2, TILES, 5)
                if there:
                    pe.wait_ge(x1_out, t + 1)
                    at_least(pe, tab_out, t if tq == 0 else t - 1)
                    pe.matmul(tab_ps[tq % 2][:, 0:TW + HEADS], x1T[:, tq, :], head_w[:, :],
                              start=True, stop=True).then_inc(tab_prod, 1)
            turns(pe, table_rows, 2, TILES, 5)

            pe.wait_ge(tab_out, TILES)
            pe.wait_ge(order_done, 2)

            def step3(i, q):
                there, g, gi, gq = item(i, q, 4)
                if there:
                    pe.wait_ge(rhs_done, g + 1)
                    pe.wait_ge(hot3_w, g + 1)
                    for u in range(4):
                        s = 4 * gq + u
                        at_least(pe, added3, 4 * (g - 1) + u + 1)
                        last = pe.matmul(bank[u][:, 0:AW], hot[:, s, :], arhs[:, s, :], start=True, stop=True)
                        last.then_inc(summed3, 1)
                there, g, _, gq = item(i, q, 1)
                if there:
                    look_up(g, gq, tile_ids(PE, by_src, g), el_tab, HEADS, hotT3, z_done, looked3)
                there, g, _, gq = item(i, q, 0)
                if there:
                    turn_hot(g, gq, hot3, hotT3, turnT3)
            turns(pe, step3, 4)

        @block.scalar
        def _(act):
            def square_roots(n, first, last):
                act.wait_ge(stats_done, n + 1)
                act.activation(rstd[:, first:last], mv[:, first:last, 1], ACT.Sqrt,
                               bias=eps_col[:, 0:1]).then_inc(sqrt_done, 1)

            def turned_out(i, q, phase):
                there, t, _, tq = item(i, q, 0, TILES, 5)
                if there:
                    act.wait_ge(turned, t + 1 + phase * TILES)
                    if phase == 0:
                        at_least(act, root_prod, t - 4)
                    elif phase == 1:
                        at_least(act, y_prod, (t - 4 + TILES) * YC)
                    else:
                        at_least(act, x1_prod, t - 4)
                    ps = turn3_ps[tq % 2] if phase == 3 else turn_ps
                    act.activation(hT[:, tq, :], ps[:, 0:D], ACT.Relu).then_inc(hT_done, 1)

            def feed_tile(i, q, phase):
                there, t, _, tq = item(i, q, -2, TILES, 5)
                if there:
                    if phase == 0 and isinstance(i, int) and i == 0 and t <= 5:
                        act.wait_ge(normed, t + 1 if t < 5 else TILES)
                    act.activation(feed[:, tq, :], acc[:, node_tile(t)], ACT.Copy).then_inc(fed, 1)

            def pieces_out(i, q, layer, beside=None):
                there, t, _, tq = item(i, q, 1, TILES, 5)
                if there:
                    for n in range(YC):
                        if beside:
                            beside(n)
                        act.wait_ge(y_prod, (t + layer * TILES) * YC + n + 1)
                        at_least(act, y_stored[n], 16 * (t + layer * TILES))
                        act.activation(ystage[:, n, :], bank[n % 2][:, :], ACT.Copy).then_inc(y_out, 1)
                    if layer == 0:
                        act.wait_ge(root_prod, t + 1)
                        act.sem_inc(act_passed, 1)
                        act.activation(acc[:, node_tile(t)], root_ps[:, 0:D], ACT.Copy).then_inc(root_out, 1)

            def high_lanes(c4, b, o, g):
                act.wait_ge(perm_lane, c4 + 1)
                for u in range(4):
                    last = act.activation(lanes_hi[:, b, :, u], lanes[:, b, :, u], ACT.Copy,
                                          scale=o.hi[:, bass.ds(4 * g + u, 1)])
                if o is by_src:
                    for u in range(4):
                        last = act.activation(lanes_lo[:, b, :, u], lanes[:, b, :, u], ACT.Copy,
                                              scale=o.lo[:, bass.ds(4 * g + u, 1)])
                last.then_inc(perm_hi, 1)

            act.wait_ge(const_done, 1)
            act.activation(warm[:, :], eps_col[:, :], ACT.Sqrt)
            square_roots(0, 0, 5)

            def layer1(i, q):
                turned_out(i, q, 0)
                pieces_out(i, q, 0)
                feed_tile(i, q, 0)
            feed_tile(0, -2, 0)
            feed_tile(0, -1, 0)
            for q in range(5):
                layer1(0, q)
                if q == 2:
                    square_roots(1, 5, TILES)
            with act.Fori(1, PLAIN_TURNS + 2) as i:
                for q in range(5):
                    layer1(i, q)
            _, blocks, first = BESIDE[PLAIN_TURNS + 2]

            def beside(q, n):
                for c4 in block_numbers(q, n, blocks, first):
                    high_lanes(c4, c4 % 4, by_dst, c4 + SCATTERED)
            for q in range(5):
                turned_out(PLAIN_TURNS + 2, q, 0)
                pieces_out(PLAIN_TURNS + 2, q, 0, lambda n: beside(q, n))
                feed_tile(PLAIN_TURNS + 2, q, 0)
            layer1(TILES // 5, 0)
            with act.Fori(PERM_BESIDE // 4, DST_BLOCKS // 4) as i:
                for b in range(4):
                    high_lanes(4 * i + b, b, by_dst, 4 * i + b + SCATTERED)

            def hot_turned(g, gq, turned_, used):
                act.wait_ge(turned_, g + 1)
                at_least(act, used, g - 1)
                return act.activation(hotT[:, gq % 2, :], turn16[gq % 2][:, 0:512], ACT.Copy)

            def step1(i, q):
                there, g, _, gq = item(i, q, 0)
                if there:
                    hot_turned(g, gq, turnT, looked).then_inc(hotT_done, 1)
                there, g, _, gq = item(i, q, 2)
                if there:
                    act.wait_ge(picked, g + 1)
                    at_least(act, summed1, g - 3)
                    for u in range(4):
                        last = act.activation(hot[:, 4 * gq + u, :], hot16[:, 4 * gq + u, :], ACT.Copy,
                                              scale=weight[:, bass.ds(4 * g + u, 1)])
                    last.then_inc(hot_w, 1)
            turns(act, step1, 2)

            def layer2(i, q):
                turned_out(i, q, 1)
                pieces_out(i, q, 1)
                feed_tile(i, q, 1)
            act.wait_ge(added1, CHUNKS)
            feed_tile(0, -2, 1)
            feed_tile(0, -1, 1)
            for q in range(5):
                layer2(0, q)
            with act.Fori(1, TILES // 5 - 1) as i:
                for q in range(5):
                    layer2(i, q)
            for q in range(5):
                layer2(TILES // 5 - 1, q)
            layer2(TILES // 5, 0)

            def step2(i, q):
                high_lanes(4 * i + q + DST_BLOCKS, q, by_src, 4 * i + q)
                there, t = root_tile(i)
                if there and q == 0:
                    act.activation(feed[:, 0, :], acc[:, node_tile(t)], ACT.Copy).then_inc(fed, 1)
                if there and q == 2:
                    act.wait_ge(turned, t + 1 + 2 * TILES)
                    at_least(act, root_prod, t + TILES)
                    act.activation(hT[:, 0, :], bank[5][:, 0:D], ACT.Relu).then_inc(hT_done, 1)
            turns(act, step2, 0, peel=2)

            square_roots(2, 0, 5)

            def table_rows(i, q):
                turned_out(i, q, 3)
                there, t, _, tq = item(i, q, 1, TILES, 5)
                if there:
                    act.wait_ge(x1_prod, t + 1)
                    at_least(act, tab_prod, t - 4)
                    act.activation(x1T[:, tq, :], x1_ps[tq % 2][0:OD, 0:P], ACT.Copy).then_inc(x1_out, 1)
                there, t, _, tq = item(i, q, 2, TILES, 5)
                if there:
                    act.wait_ge(tab_prod, t + 1)
                    act.activation(tabst[:, bass.ds(t, 1), :].rearrange("p a c -> p (a c)"),
                                   tab_ps[tq % 2][:, 0:TW], ACT.Copy)
                    act.activation(el_tab[:, node_tile(t, HEADS)], tab_ps[tq % 2][:, TW:TW + HEADS],
                                   ACT.Copy).then_inc(tab_out, 1)
            for q in range(5):
                table_rows(0, q)
            square_roots(3, 5, TILES)
            for q in range(5):
                table_rows(1, q)
            with act.Fori(2, TILES // 5) as i:
                for q in range(5):
                    table_rows(i, q)
            table_rows(TILES // 5, 0)
            table_rows(TILES // 5, 1)

            def step3(i, q):
                there, g, _, gq = item(i, q, 2)
                if there:
                    act.wait_ge(z_done, g + 1)
                    at_least(act, summed3, 4 * (g - 3))
                    act.activation(arhs[:, 4 * gq:4 * gq + 4, D:AW], zbuf[:, gq, :, :], ACT.Exp).then_inc(e_done, 1)
                    act.activation(hot[:, 4 * gq:4 * gq + 4, :], hot16[:, 4 * gq:4 * gq + 4, :],
                                   ACT.Copy).then_inc(hot3_w, 1)
                there, g, _, gq = item(i, q, 0)
                if there:
                    hot_turned(g, gq, turnT3, looked3).then_inc(hotT3, 1)
            turns(act, step3, 2)

            for n in range(5):
                act.wait_ge(value_done, n + 1)
                at_least(act, out_done, n - 1)
                e5 = expo[:, (n % 2) * 5 * D:(n % 2 + 1) * 5 * D].rearrange("p (t d) -> p t d", t=5)
                v5 = acc[:, :].rearrange("p (t c) -> p t c", c=AW)[:, 5 * n:5 * n + 5, 0:D]
                act.activation(e5, v5, ACT.Relu, scale=-1.0).then_inc(below, 1)
                act.wait_ge(below, n + 1)
                act.activation(e5, e5, ACT.Exp, scale=-1.0).then_inc(exp_done, 1)

        @block.vector
        def _(dve):
            linked = [0]

            def link(ins):
                linked[0] += 1
                ins.then_inc(dve_link, 1)
                dve.wait_ge(dve_link, linked[0])

            def norm_tiles(n, first, last, place_):
                with dve.Fori(first // 5, last // 5) as i:
                    for q in range(5):
                        t = 5 * i + q
                        dve.bn_stats(stats[:, bass.ds(t, 1), :].rearrange("p a b -> p (a b)"), xb[:, node_tile(t)])
                link(dve.drain())
                for t in range(first, last):
                    dve.bn_aggr(mv[:, t, :], stats[:, t, :])
                link(dve.drain())
                dve.nop().then_inc(stats_done, 1)
                dve.wait_ge(sqrt_done, n + 1)
                link(dve.reciprocal(rstd[:, first:last], rstd[:, first:last]))

                def normalise(i, q):
                    t = 5 * i + q
                    to, signal = place_(t, q)
                    dve.tensor_scalar(to, xb[:, node_tile(t)],
                                      mv[:, bass.ds(t, 1), 0:1].rearrange("p a b -> p (a b)"),
                                      rstd[:, bass.ds(t, 1)], ALU.subtract, ALU.mult).then_inc(signal, 1)
                with dve.Fori(first // 5, last // 5) as i:
                    for q in range(5):
                        normalise(i, q)

            def to_acc(t, q):
                return acc[:, node_tile(t)], normed

            def to_feed(t, q):
                dve.wait_ge(turned, t - 4 + 3 * TILES)
                return feed[:, q, :], fed

            real = slice(0, EC)

            def conv_row():
                link(dve.scalar_tensor_tensor(out=tmp_i[:, real], in0=src_i[:, :], scalar=float(R), in1=et_i[:, :],
                                              op0=ALU.mult, op1=ALU.add))
                return tmp_i[:, real]

            def count(n, o, key, payload):
                link(dve.tensor_scalar(tmp_i[:, real], key, SHIFT, None, ALU.arith_shift_right))
                link(dve.tensor_copy(tile_f[:, real], tmp_i[:, real]))
                at_least(dve, counts_summed, n)
                for k in range(TILES):
                    dve.tensor_scalar(o.member[:, k, :], tile_f[:, :], float(k), None, ALU.is_equal, ALU.add,
                                      accum_out=n_in[:, k:k + 1])
                link(dve.drain())
                dve.nop().then_inc(counts_ready, 1)
                link(dve.tensor_scalar(low_i[:, real], key, P - 1, None, ALU.bitwise_and))
                if n == 0:
                    link(dve.tensor_copy(low16[:, real], low_i[:, real]))
                    link(dve.scalar_tensor_tensor(out=tile_rel[:, real], in0=tile_f[:, real], scalar=float(R),
                                                  in1=et_i[:, :], op0=ALU.mult, op1=ALU.add))
                row = payload()
                if n == 0:
                    part, whole = slice(0, 4 * (SCATTERED + 1)), scatter_list[:, :, 1]
                    link(dve.scalar_tensor_tensor(out=whole, in0=row[:, part], scalar=float(P), in1=low_i[:, part],
                                                  op0=ALU.mult, op1=ALU.add))
                    link(dve.tensor_scalar(whole, whole, 1.0, None, ALU.add))
                link(dve.tensor_scalar(tmp2_i[:, real], row, 4, None, ALU.arith_shift_right))
                link(dve.tensor_copy(o.hi[:, real], tmp2_i[:, real]))
                link(dve.tensor_scalar(tmp2_i[:, real], row, 15, None, ALU.bitwise_and))
                link(dve.scalar_tensor_tensor(out=pos[:, real], in0=tmp2_i[:, real], scalar=float(P),
                                              in1=low_i[:, real], op0=ALU.mult, op1=ALU.add))
                link(dve.tensor_scalar(o.lo[:, real], pos[:, real], 1.0, None, ALU.add))

            def place(n, o):
                dve.wait_ge(counts_summed, n + 1)
                link(dve.tensor_scalar(tot_i[:, :], count_ps[:, 0:TILES], float(P - 1), None, ALU.add))
                link(dve.tensor_scalar(tot_i[:, :], tot_i[:, :], SHIFT, None, ALU.arith_shift_right))
                link(dve.tensor_copy(nch[:, :], tot_i[:, :]))
                link(dve.tensor_tensor_scan(cend[:, :], nch[:, :], zeros16[:, 0:TILES], 0.0, ALU.add, ALU.add))
                link(dve.tensor_tensor(start[:, :], cend[:, :], nch[:, :], ALU.subtract))
                link(dve.scalar_tensor_tensor(out=start[:, :], in0=start[:, :], scalar=float(P),
                                              in1=count_ps[:, TILES:2 * TILES], op0=ALU.mult, op1=ALU.add))
                dve.nop().then_inc(counts_read, 1)
                link(dve.tensor_scalar(start[:, :], start[:, :], -1.0, None, ALU.add))
                link(dve.memset(pos[:, :], -1.0))
                link(dve.memset(tid_f[:, :], 0.0))
                base = linked[0]

                def scan(k):
                    if k >= 2:
                        dve.wait_ge(dve_link, base + 3 * k - 3)
                    linked[0] += 1
                    dve.tensor_tensor_scan(run[:, k % 2, :], o.member[:, k, :], zeros16[0:EP, :],
                                           start[0:EP, k:k + 1], ALU.add, ALU.add).then_inc(dve_link, 1)
                scan(0)
                for k in range(TILES):
                    if k + 1 < TILES:
                        scan(k + 1)
                    dve.wait_ge(dve_link, base + max(3 * k, 1))
                    linked[0] += 1
                    dve.copy_predicated(pos[:, :], o.member[:, k, :], run[:, k % 2, :]).then_inc(dve_link, 1)
                    if k:
                        dve.wait_ge(dve_link, base + 3 * k + 1)
                    linked[0] += 1
                    dve.scalar_tensor_tensor(out=tid_f[:, :], in0=iota16[0:1, 0:CHUNKS], scalar=cend[0:1, k:k + 1],
                                             in1=tid_f[:, :], op0=ALU.is_ge, op1=ALU.add).then_inc(dve_link, 1)
                dve.wait_ge(dve_link, linked[0])
                link(dve.tensor_scalar(o.tid[:, :], tid_f[:, :], float(TILES - 1), None, ALU.min))
                link(dve.tensor_copy(tmp_i[:, :], pos[:, :]))
                link(dve.tensor_scalar(tmp2_i[:, :], tmp_i[:, :], SHIFT, None, ALU.arith_shift_right))
                link(dve.tensor_copy(o.chunk[:, :], tmp2_i[:, :]))
                link(dve.tensor_scalar(tmp2_i[:, :], tmp_i[:, :], P - 1, None, ALU.bitwise_and))
                link(dve.tensor_copy(o.lane[:, :], tmp2_i[:, :]))
                if n == 0:
                    part = slice(0, 4 * (SCATTERED + 1))
                    dve.scalar_tensor_tensor(out=scatter_list[:, :, 0], in0=tmp2_i[:, part], scalar=float(CHUNKS),
                                             in1=o.chunk[:, part], op0=ALU.mult, op1=ALU.add).then_inc(scatter_ready, 1)

            def four(columns, g):
                return columns[:, bass.ds(4 * g, 4)].unsqueeze(1).broadcast_to([EP, P, 4])

            def columns(c4, b, o, g):
                at_least(dve, perm_used, c4 - 3)
                dve.tensor_tensor(lanes[:, b, :, :], iota4[0:EP, :, :], four(o.lane, g),
                                  ALU.is_equal).then_inc(perm_lane, 1)
                for u in range(4):
                    last = dve.tensor_scalar(wide[:, 4 * b + u, :], iota16[0:EP, 0:CHUNKS],
                                             o.chunk[:, bass.ds(4 * g + u, 1)], None, ALU.is_equal)
                if o is by_dst:
                    dve.wait_ge(perm_lane, c4 + 1)
                    last = dve.tensor_tensor(lanes_lo[:, b, :, :], lanes[:, b, :, :], four(o.lo, g), ALU.mult)
                last.then_inc(perm_ready, 1)

            def finish_order(o, n):
                dve.wait_ge(perm_used, DST_BLOCKS + GROUPS * n)
                hi, lo = perm_ps[0][:, 0:CHUNKS], perm_ps[1][:, 0:CHUNKS]
                link(dve.tensor_copy(empty[:, :], lo))
                link(dve.scalar_tensor_tensor(out=slot2_i[:, :], in0=hi, scalar=float(16 * P), in1=empty[:, :],
                                              op0=ALU.mult, op1=ALU.add))
                if n == 0:
                    dve.wait_ge(slots_in, 16)
                    link(dve.tensor_tensor(slot2_i[:, :], slot2_i[:, :], slot_i[:, :], ALU.add))
                link(dve.tensor_scalar(slot_i[:, :], slot2_i[:, :], -1.0, 0.0, ALU.add, ALU.max))
                link(dve.tensor_scalar(o.idx[:, 0:CHUNKS], slot_i[:, :], SHIFT, None, ALU.arith_shift_right))
                dve.nop().then_inc(idx_done, 1)
                link(dve.tensor_scalar(empty[:, :], slot2_i[:, :], 0.0, None, ALU.is_equal))
                link(dve.tensor_scalar(slot2_i[:, :], slot_i[:, :], P - 1, None, ALU.bitwise_and))
                link(dve.scalar_tensor_tensor(out=o.loc[:, :], in0=empty[:, :], scalar=-float(P), in1=slot2_i[:, :],
                                              op0=ALU.mult, op1=ALU.add))
                if n == 0:
                    link(dve.tensor_scalar(slot2_i[:, :], o.idx[:, 0:CHUNKS], R - 1, None, ALU.bitwise_and))
                    link(dve.tensor_copy(et_f[:, :], slot2_i[:, :]))
                dve.nop().then_inc(order_done, 1)

            link(dve.memset(zeros16[:, :], 0.0))
            link(dve.memset(xb[:, (TILES - 1) * D:], 0.0))
            link(dve.memset(eps_col[:, :], EPS_LN))
            link(dve.memset(slot_i[:, :], 0))
            link(dve.memset(ones[:, :], 1.0))
            link(dve.memset(tile_f[:, :], -1.0))
            for o in orders:
                link(dve.memset(o.hi[:, :], 0.0))
                link(dve.memset(o.lo[:, :], 0.0))
                link(dve.memset(o.idx[:, CHUNKS:], 0))
            dve.wait_ge(pool_const, 3)
            link(dve.tensor_scalar(ident[:, :], iota16[:, 0:P], lane_no[:, 0:1], None, ALU.is_equal))
            link(dve.tensor_scalar(ident16[:, :], iota16[:, 0:P], lane_no[:, 0:1], None, ALU.is_equal))
            link(dve.tensor_scalar(before[:, :], iota16[:, 0:P], lane_no[:, 0:1], None, ALU.is_gt))
            link(dve.tensor_scalar(head_w[:, 0:OD], iota16[0:OD, 0:OD], lane_no[0:OD, 0:1], None, ALU.is_equal))
            dve.nop().then_inc(const_done, 1)

            dve.wait_ge(x_first, 16)
            norm_tiles(0, 0, 5, to_acc)
            dve.wait_ge(e_in, 48)
            count(0, by_dst, dst_i[:, :], conv_row)
            dve.wait_ge(x_in, 32)
            norm_tiles(1, 5, TILES, to_acc)
            place(0, by_dst)
            dve.wait_ge(b_in, 48)

            def hist_block(i, b):
                g = 4 * i + b
                at_least(dve, hist_used, g - 3)
                dve.tensor_tensor(lanes[:, b, :, :], iota4[0:EP, :, :], four(low16, g), ALU.is_equal)
                for u in range(4):
                    last = dve.tensor_scalar(wide[:, 4 * b + u, 0:HC], iota16[0:EP, 0:HC],
                                             tile_rel[:, bass.ds(4 * g + u, 1)], None, ALU.is_equal)
                last.then_inc(hist_ready, 1)
            turns(dve, hist_block, 0, EC // 4, 4)

            dve.wait_ge(hist_used, EC // 4)
            def permute_dst(i, q):
                columns(4 * i + q, q, by_dst, 4 * i + q + SCATTERED)
            turns(dve, permute_dst, 0, DST_BLOCKS - 4)
            link(dve.tensor_scalar(rcnt[:, :], hist_ps[:, 0:HC], 1.0, None, ALU.max))
            link(dve.reciprocal(rcnt[:, :], rcnt[:, :]))
            dve.nop().then_inc(rcnt_done, 1)

            def bias_tile(i, q):
                t = 5 * i + q
                dve.wait_ge(root_out, t + 1)
                at_tile = acc[:, node_tile(t)]
                dve.tensor_tensor(at_tile, at_tile, bias1[:, :], ALU.add)
            turns(dve, bias_tile, 0, TILES, 5)
            for q in range(4):
                permute_dst(DST_BLOCKS // 4 - 1, q)
            finish_order(by_dst, 0)

            def add_sum(g, u, ids, source, added, target, width):
                at_least(dve, added, 4 * g + u)
                to = target[:, node_tile(ids[u], width)]
                dve.tensor_tensor(to, source, to, ALU.add).then_inc(added, 1)

            def conv_sum(gq, u):
                return bank[2 * (gq % 2) + u // 2][:, (u % 2) * D:(u % 2 + 1) * D]

            def step1(i, q):
                there, g, _, gq = item(i, q, 0)
                if there:
                    at_least(dve, hot_w, g - 3)
                    for u in range(4):
                        last = dve.tensor_scalar(hot16[:, 4 * gq + u, :], iota16[:, 0:P],
                                                 by_dst.loc[:, bass.ds(4 * g + u, 1)], None, ALU.is_equal)
                    last.then_inc(hot_ready, 1)
                there, g, _, gq = item(i, q, 2)
                if there:
                    dve.wait_ge(looked, g + 1)
                    at_least(dve, picked, g)
                    for u in range(4):
                        last = dve.scalar_tensor_tensor(out=trash[:, u, :], in0=iota16[:, 0:R],
                                                        scalar=et_f[:, bass.ds(4 * g + u, 1)],
                                                        in1=bank[4 + gq % 2][:, u * R:(u + 1) * R], op0=ALU.is_equal,
                                                        op1=ALU.mult, accum_out=weight[:, bass.ds(4 * g + u, 1)])
                    last.then_inc(picked, 1)
                there, g, _, gq = item(i, q, 4)
                if there:
                    ids = tile_ids(DVE, by_dst, g)
                    dve.wait_ge(summed1, g + 1)
                    for u in range(4):
                        add_sum(g, u, ids, conv_sum(gq, u), added1, acc, D)
            turns(dve, step1, 4)

            dve.wait_ge(added1, CHUNKS)
            count(1, by_src, src_i[:, :], lambda: dst_i[:, :])
            place(1, by_src)

            with dve.Fori(0, TILES // 5) as i:
                for q in range(5):
                    at_tile = xb[:, node_tile(5 * i + q)]
                    dve.tensor_tensor(at_tile, at_tile, bias2[:, :], ALU.add)
            link(dve.drain())

            def step2(i, q):
                here, g, _, gq = item(i, q, 0)
                there2, g2, _, gq2 = item(i, q, 2)
                if there2:
                    ids = tile_ids(DVE, by_dst, g2)
                if here:
                    at_least(dve, summed2, g - 3)
                rooted, t = root_tile(i, 1)
                rooted = rooted and q == 0
                if rooted:
                    dve.wait_ge(root_prod, t + 1 + TILES)
                    dve.wait_ge(added2, 4 * g2)
                    dve.tensor_tensor(xb[:, node_tile(t)], bank[4][:, 0:D], xb[:, node_tile(t)],
                                      ALU.add).then_inc(root_out, 1)
                if there2:
                    dve.wait_ge(summed2, g2 + 1)
                for u in range(4):
                    if here:
                        last = dve.tensor_scalar(hot[:, 4 * gq + u, :], iota16[:, 0:P],
                                                 by_dst.loc[:, bass.ds(4 * g + u, 1)],
                                                 weight[:, bass.ds(4 * g + u, 1)], ALU.is_equal, ALU.mult)
                        if u == 3:
                            last.then_inc(hot2, 1)
                    if rooted and u == 0:
                        dve.wait_ge(root_out, t + 1 + TILES)
                    if there2:
                        add_sum(g2, u, ids, conv_sum(gq2, u), added2, xb, D)
                if here:
                    columns(g + DST_BLOCKS, gq, by_src, g)
            turns(dve, step2, 2)
            dve.wait_ge(added2, CHUNKS)

            norm_tiles(2, 0, 5, to_feed)
            norm_tiles(3, 5, TILES, to_feed)
            finish_order(by_src, 1)

            dve.wait_ge(acc_zeroed, 1)

            def scores(g, gi, gq):
                for u in range(4):
                    dve.wait_ge(landed[4 * gq + u], 16 * (gi + 1 + 2 * TURNS))
                dve.wait_ge(looked3, g + 1)
                at_least(dve, e_done, g - 3)
                dve.tensor_tensor(zbuf[:, gq, :, :],
                                  bank[4 + gq % 2][:, 0:4 * HEADS].rearrange("p (u h) -> p u h", u=4),
                                  arows[:, 4 * gq:4 * gq + 4, OD:TW], ALU.add).then_inc(z_sum, 1)
                dve.wait_ge(z_sum, g + 1)
                zf = zbuf[:, gq, :, :].rearrange("p u h -> p (u h)")
                dve.scalar_tensor_tensor(out=zf, in0=zf, scalar=SLOPE, in1=zf, op0=ALU.mult,
                                         op1=ALU.max).then_inc(z_done, 1)

            def step3(i, q):
                here, g, _, gq = item(i, q, 0)
                there2, g2, gi2, gq2 = item(i, q, 2)
                there3, g3, _, gq3 = item(i, q, 3)
                there5, g5, _, gq5 = item(i, q, 5)
                if there5:
                    ids = tile_ids(DVE, by_src, g5)
                if here:
                    at_least(dve, hot3_w, g - 3)
                for u in range(4):
                    if here:
                        ins = dve.tensor_scalar(hot16[:, 4 * gq + u, :], iota16[:, 0:P],
                                                by_src.loc[:, bass.ds(4 * g + u, 1)], None, ALU.is_equal)
                        if u == 3:
                            ins.then_inc(hot3, 1)
                    if there5:
                        dve.wait_ge(summed3, 4 * g5 + u + 1)
                        add_sum(g5, u, ids, bank[u][:, 0:AW], added3, acc, AW)
                    if there3:
                        s = 4 * gq3 + u
                        dve.wait_ge(e_done, g3 + 1)
                        ins = dve.tensor_tensor(
                            arhs[:, s, 0:D].rearrange("p (h o) -> p h o", h=HEADS),
                            arows[:, s, 0:OD].unsqueeze(1).broadcast_to([P, HEADS, OD]),
                            arhs[:, s, D:AW].unsqueeze(2).broadcast_to([P, HEADS, OD]), ALU.mult)
                        if u == 3:
                            ins.then_inc(rhs_done, 1)
                    if there2 and u == 1:
                        scores(g2, gi2, gq2)
            turns(dve, step3, 5)

            dve.wait_ge(added3, CHUNKS)
            av = acc[:, :].rearrange("p (t c) -> p t c", c=AW)
            rsum = tabst[:, :, 0:HEADS]
            dve.wait_ge(tab_stored, 80)
            link(dve.tensor_scalar(rsum, av[:, :, D:AW], EPS_ROW, None, ALU.max))
            link(dve.reciprocal(rsum, rsum))
            for n in range(6):
                if n < 5:
                    ts = slice(5 * n, 5 * n + 5)
                    v = av[:, ts, 0:D].rearrange("p t (h o) -> p t h o", h=HEADS)
                    link(dve.tensor_tensor(v, v, rsum[:, ts, :].unsqueeze(3).broadcast_to([P, 5, HEADS, OD]), ALU.mult))
                    dve.tensor_tensor(v, v, biasg[:, :].unsqueeze(1).unsqueeze(1).broadcast_to([P, 5, HEADS, OD]),
                                      ALU.add).then_inc(value_done, 1)
                if n:
                    dve.wait_ge(exp_done, n)
                    e5 = expo[:, ((n - 1) % 2) * 5 * D:((n - 1) % 2 + 1) * 5 * D].rearrange("p (t d) -> p t d", t=5)
                    v5 = av[:, 5 * n - 5:5 * n, 0:D]
                    dve.scalar_tensor_tensor(out=e5, in0=v5, scalar=0.0, in1=e5, op0=ALU.max,
                                             op1=ALU.add).then_inc(plus_done, 1)
                if n == 5:
                    dve.wait_ge(plus_done, n)
                    dve.wait_ge(x_less_one, n)
                    xs = xb[:, 5 * n * D - 5 * D:5 * n * D]
                    dve.wait_ge(out_done, n - 1)
                    dve.tensor_tensor(xs, xs, expo[:, (n - 1) % 2 * 5 * D:((n - 1) % 2 + 1) * 5 * D],
                                      ALU.add).then_inc(out_done, 1)


_INS = ["x", "src", "dst", "edge_type_8", "L0_gnn_W1", "L0_gnn_Wroot1", "L0_gnn_b1", "L0_gnn_W2", "L0_gnn_Wroot2",
        "L0_gnn_b2", "L1_gnn_W", "L1_gnn_Wl", "L1_gnn_Wr", "L1_gnn_b"]


def kernel(**inputs):
    import concourse.bacc as bacc
    from concourse.bass_utils import run_bass_kernel_spmd

    nc = bacc.Bacc("TRN2", target_bir_lowering=False, num_devices=1)
    arrays, args = {}, []
    for name in _INS:
        a = np.ascontiguousarray(inputs[name])
        arrays[f"in_{name}"] = a
        args.append(nc.dram_tensor(f"in_{name}", a.shape, mybir.dt.from_np(a.dtype), kind="ExternalInput").ap())
    shape = inputs["x"].shape
    args.append(nc.dram_tensor("out_0", shape, F32, kind="ExternalOutput").ap())
    build_gnn(nc, *args)
    r = run_bass_kernel_spmd(nc, [arrays], core_ids=[0])
    return r.results[0]["out_0"]
```
